# Optimizing a Trainium2 kernel written in Bass

```python
import numpy as np
import jax
import jax.numpy as jnp

def _softmax(x, axis=-1):
    return jax.nn.softmax(x, axis=axis)

def _gelu(x):
    return jax.nn.gelu(x, approximate=True)

def _silu(x):
    return jax.nn.silu(x)

def _sigmoid(x):
    return jax.nn.sigmoid(x)

def _layernorm(x, axis=-1, eps=1e-05):
    m = jnp.mean(x, axis=axis, keepdims=True)
    v = jnp.var(x, axis=axis, keepdims=True)
    return (x - m) / jnp.sqrt(v + eps)

def _scatter_add(tgt, idx, src, axis=0):
    return tgt.at[idx].add(src)

def _segment_sum(src, seg, n):
    return jax.ops.segment_sum(src, seg, n)
kernel_name = 'mk_xattn_ffn_d1_seqx_r8_f685d3'

def setup_inputs(seed: int=0):
    np.random.seed(seed)
    _w = jnp.asarray

    def _rec_inputs():
        import jax
        import jax.numpy as jnp
        _rk = jax.random.key(seed)
        x = 0.5 + 0.2887 * jax.random.normal(jax.random.fold_in(_rk, 1), (4, 256, 256), jnp.float32)
        _lenS = 256 - jax.random.randint(jax.random.fold_in(_rk, 7), (4,), 0, max(1, 256 // 4) + 1, jnp.int32)
        _lenS2 = 256 - jax.random.randint(jax.random.fold_in(_rk, 8), (4,), 0, max(1, 256 // 4) + 1, jnp.int32)
        _ctx_512P = jax.random.normal(jax.random.fold_in(_rk, 11), (4, 16, 64), jnp.float32)
        _ctx_512c = jax.random.dirichlet(jax.random.fold_in(_rk, 511), 0.3 * jnp.ones((16,), jnp.float32), (4, 256))
        _ctx_512t = jnp.einsum('bsk,bkd->bsd', _ctx_512c, _ctx_512P)
        _ctx_512t = _ctx_512t * jax.lax.rsqrt(jnp.mean(jnp.square(_ctx_512t)) + 1e-12) * 0.953939
        ctx_512 = -0.000392918 + 0.999932 * (_ctx_512t + 0.3 * jax.random.normal(jax.random.fold_in(_rk, 611), (4, 256, 64), jnp.float32))
        return (x, ctx_512)
    x, ctx_512 = _rec_inputs()

    def _L0_xattn_setup():
        import jax, jax.numpy as jnp
        import numpy as np
        B, N, D = (16, 256, 64)
        H = 4
        TOP_K_RATIO = 0.3
        key = jax.random.key(seed)
        k1, k2, k3, k4 = jax.random.split(key, 4)
        h = jax.random.normal(k1, (B, N, D), dtype=jnp.float32)
        adj_raw = jax.random.uniform(k2, (B, N, N), dtype=jnp.float32)
        lim = 1.0 / np.sqrt(D)
        Wq = jax.random.uniform(k3, (D, D), minval=-lim, maxval=lim, dtype=jnp.float32)
        Wk = jax.random.uniform(k4, (D, D), minval=-lim, maxval=lim, dtype=jnp.float32)
        gamma_raw = jnp.float32(-0.85)
        return {'h': h, 'adj_raw': adj_raw, 'Wq': Wq, 'Wk': Wk, 'gamma_raw': gamma_raw}
    _L0_xattn_all = _L0_xattn_setup()
    _L0_xattn_in = {k: v for k, v in _L0_xattn_all.items() if k in ('Wq', 'Wk', 'gamma_raw')}
    del _L0_xattn_all

    def _L0_ffn_setup():
        import jax, jax.numpy as jnp
        import numpy as np
        B, S, DIM = (2, 256, 256)
        INTER = 128
        E = 8
        K = 2
        N_SHARED = 1
        ROUTE_SCALE = 1.0
        key = jax.random.key(seed)
        ks = jax.random.split(key, 8)
        s_in = 1.0 / np.sqrt(DIM)
        s_hid = 1.0 / np.sqrt(INTER)
        return {'x': jax.random.normal(ks[0], (B, S, DIM), dtype=jnp.float32), 'gate_w': jax.random.normal(ks[1], (E, DIM), dtype=jnp.float32) * s_in, 'w1': jax.random.normal(ks[2], (E, INTER, DIM), dtype=jnp.float32) * s_in, 'w2': jax.random.normal(ks[3], (E, DIM, INTER), dtype=jnp.float32) * s_hid, 'w3': jax.random.normal(ks[4], (E, INTER, DIM), dtype=jnp.float32) * s_in, 'ws1': jax.random.normal(ks[5], (N_SHARED * INTER, DIM), dtype=jnp.float32) * s_in, 'ws2': jax.random.normal(ks[6], (DIM, N_SHARED * INTER), dtype=jnp.float32) * s_hid, 'ws3': jax.random.normal(ks[7], (N_SHARED * INTER, DIM), dtype=jnp.float32) * s_in}
    _L0_ffn_all = _L0_ffn_setup()
    _L0_ffn_in = {k: v for k, v in _L0_ffn_all.items() if k in ('gate_w', 'w1', 'w2', 'w3', 'ws1', 'ws2', 'ws3')}
    del _L0_ffn_all
    return {'x': x, 'ctx_512': ctx_512, 'L0_xattn_Wq': _L0_xattn_in['Wq'], 'L0_xattn_Wk': _L0_xattn_in['Wk'], 'L0_xattn_gamma_raw': _L0_xattn_in['gamma_raw'], 'L0_ffn_gate_w': _L0_ffn_in['gate_w'], 'L0_ffn_w1': _L0_ffn_in['w1'], 'L0_ffn_w2': _L0_ffn_in['w2'], 'L0_ffn_w3': _L0_ffn_in['w3'], 'L0_ffn_ws1': _L0_ffn_in['ws1'], 'L0_ffn_ws2': _L0_ffn_in['ws2'], 'L0_ffn_ws3': _L0_ffn_in['ws3']}

def reference(x, ctx_512, L0_xattn_Wq, L0_xattn_Wk, L0_xattn_gamma_raw, L0_ffn_gate_w, L0_ffn_w1, L0_ffn_w2, L0_ffn_w3, L0_ffn_ws1, L0_ffn_ws2, L0_ffn_ws3):
    import jax
    import jax.numpy as jnp

    def _L0_xattn_ref(h, adj_raw, Wq, Wk, gamma_raw):
        import jax, jax.numpy as jnp
        import numpy as np
        B, N, D = (16, 256, 64)
        H = 4
        TOP_K_RATIO = 0.3
        b, n, dm = h.shape
        d = dm // H
        Q = (h @ Wq.T).reshape(b, n, H, d).transpose(0, 2, 1, 3)
        K = (h @ Wk.T).reshape(b, n, H, d).transpose(0, 2, 1, 3)
        sim = jnp.einsum('bhnd,bhmd->bnm', Q, K) / (jnp.sqrt(jnp.float32(d)) * H)
        k = max(1, int(n * TOP_K_RATIO))
        topk_vals = jax.lax.top_k(sim, k)[0]
        threshold = topk_vals[:, :, -1:]
        sparse_mask = (sim >= threshold).astype(sim.dtype)
        A_learned = jax.nn.sigmoid(sim) * sparse_mask
        A_learned = (A_learned + jnp.swapaxes(A_learned, -1, -2)) * 0.5
        gamma = jax.nn.sigmoid(gamma_raw)
        return (1.0 - gamma) * adj_raw + gamma * A_learned

    def _L0_ffn_ref(x, gate_w, w1, w2, w3, ws1, ws2, ws3):
        import jax, jax.numpy as jnp
        import numpy as np
        B, S, DIM = (2, 256, 256)
        INTER = 128
        E = 8
        K = 2
        N_SHARED = 1
        ROUTE_SCALE = 1.0
        shape = x.shape
        xf = x.reshape(-1, DIM)
        scores = jax.nn.softmax(xf @ gate_w.T, axis=-1)
        weights, idx = jax.lax.top_k(scores, K)
        weights = weights * ROUTE_SCALE
        h = jnp.einsum('td,eid->eti', xf, w1)
        g = jax.nn.silu(h) * jnp.einsum('td,eid->eti', xf, w3)
        eo = jnp.einsum('eti,edi->etd', g, w2)
        comb = jnp.einsum('tke,tk->te', jax.nn.one_hot(idx, E, dtype=xf.dtype), weights)
        y = jnp.einsum('etd,te->td', eo, comb)
        z = jax.nn.silu(xf @ ws1.T) * (xf @ ws3.T) @ ws2.T
        return (y + z).reshape(shape)
    x = x + _L0_xattn_ref(ctx_512, _layernorm(x, axis=-1), L0_xattn_Wq, L0_xattn_Wk, L0_xattn_gamma_raw)
    x = x + _L0_ffn_ref(_layernorm(x, axis=-1), L0_ffn_gate_w, L0_ffn_w1, L0_ffn_w2, L0_ffn_w3, L0_ffn_ws1, L0_ffn_ws2, L0_ffn_ws3)
    return x

_drawn_inputs = setup_inputs


def setup_inputs(seed=0):
    import zlib

    import numpy as np

    out = dict(_drawn_inputs(seed))
    spreads = {}
    factors = {}
    for name, (base, spread) in spreads.items():
        noise = np.random.default_rng([zlib.crc32(name.encode()), seed]).standard_normal(out[name].shape)
        drawn = base * np.exp(spread * noise) if base else spread * noise
        out[name] = jnp.asarray(drawn.astype(out[name].dtype))
    for name, factor in factors.items():
        out[name] = (out[name] * factor).astype(out[name].dtype)
    return out
```

```python
import concourse.bass as bass
from concourse import mybir
from contextlib import ExitStack

F32 = mybir.dt.float32
F32R = mybir.dt.float32r
ALU = mybir.AluOpType
ACT = mybir.ActivationFunctionType

P = 128
B = 4
N = 256
D = 256
DC = 64
HEADS = 4
T = N // P
KD = D // P
E = 8
INTER = 128
TOPK = int(N * 0.3)
SIM_SCALE = 1.0 / (float(DC // HEADS) ** 0.5 * HEADS)
LOWEST = -3.0e38
ROUNDS = (TOPK + 7) // 8
KTH = (TOPK - 1) % 8
FILL = 6
SLOTS = 1 + E // 2


def experts_of(slot):
    return [0] if slot == 0 else [2 * slot - 1, 2 * slot]


def attention_ffn(nc, x, ctxT, wqT, wkT, gamma, gateT, w1t, w3t, w2t, ws1t, ws3t, ws2t, out):
    es = ExitStack()
    with es:
        def sb(name, shape, dt=F32):
            return es.enter_context(nc.sbuf_tensor(name, shape, dt))

        def pb(name):
            return es.enter_context(nc.psum_tensor(name, [P, 512], F32))

        def sem(name):
            return es.enter_context(nc.semaphore(name))

        x_sb = sb("x_sb", [P, B, T, D])
        ctx_sb = sb("ctx_sb", [DC, B * N])
        wqk_sb = sb("wqk_sb", [DC, 2, DC])
        gamma_sb = sb("gamma_sb", [P, 1])
        gate_sb = sb("gate_sb", [P, KD, E])
        gate_r = sb("gate_r", [P, KD, 2, E], F32R)
        up_raw = sb("up_raw", [P, 1 + E, 2, KD, INTER])
        up_hi = sb("up_hi", [P, 1 + E, 2, KD, INTER], F32R)
        up_lo = sb("up_lo", [P, 1 + E, 2, KD, INTER], F32R)
        dn_raw = sb("dn_raw", [P, 1 + E, D])
        dn_hi = sb("dn_hi", [P, 1 + E, D], F32R)
        dn_lo = sb("dn_lo", [P, 1 + E, D], F32R)
        ident = sb("ident", [P, P])
        pick = sb("pick", [2 * E, E, P])
        pick_r = sb("pick_r", [2 * E, E, P], F32R)
        minus_half = sb("minus_half", [P, T])
        euler = sb("euler", [P, T, E])
        g_tanh = sb("g_tanh", [P, 1])
        g_rest = sb("g_rest", [P, 1])
        g_quarter = sb("g_quarter", [P, 1])

        qkT = sb("qkT", [DC, 2, N])
        scores = sb("scores", [P, T, N])
        left = sb("left", [P, T, N])
        top8 = sb("top8", [P, T, 8])
        sig = sb("sig", [P, T, N])
        masked = sb("masked", [P, T, N])
        st1 = sb("st1", [P, T, 6])
        mv1 = sb("mv1", [P, T, 2])
        var1 = sb("var1", [P, T])
        rs1 = sb("rs1", [P, T])
        c1 = sb("c1", [P, T])
        sc1 = sb("sc1", [P, T])
        mc1 = sb("mc1", [P, T])
        bi1 = sb("bi1", [P, T])
        ln1 = sb("ln1", [P, T, N])
        base = sb("base", [P, T, N])
        x1 = [sb(f"x1_{i}", [P, T, D]) for i in range(2)]
        st2 = sb("st2", [P, T, 6])
        mv2 = sb("mv2", [P, T, 2])
        var2 = sb("var2", [P, T])
        rs2 = sb("rs2", [P, T])
        z = sb("z", [P, T, D])
        z_hi = [sb(f"z_hi{i}", [P, KD, N], F32R) for i in range(2)]
        z_lo = [sb(f"z_lo{i}", [P, KD, N], F32R) for i in range(2)]

        lgx = sb("lgx", [P, T, E + FILL])
        lgp = sb("lgp", [P, T, 2, E])
        lg8 = sb("lg8", [P, T, 8])
        take = sb("take", [P, T, 8])
        rest = sb("rest", [P, T, E + FILL])
        lgd = sb("lgd", [P, T, E])
        ex = sb("ex", [P, T, E])
        exs = sb("exs", [P, T])
        exr = sb("exr", [P, T])
        chosen = sb("chosen", [P, T, E])
        exc = sb("exc", [P, T, E])
        comb = sb("comb", [P, T, E])
        comb_r = sb("comb_r", [P, T, 2, E], F32R)
        combT = sb("combT", [2 * E, N], F32R)

        sil = [sb(f"sil{i}", [P, 512]) for i in range(2)]
        prod = sb("prod", [P, 512])
        gc = [sb(f"gc{i}", [P, 512]) for i in range(2)]
        g_hi = [sb(f"g_hi{i}", [P, 512], F32R) for i in range(3)]
        g_lo = [sb(f"g_lo{i}", [P, 512], F32R) for i in range(3)]
        fin = [sb(f"fin{b}", [P, T, D]) for b in range(B)]

        ps_a = pb("ps_a")
        ps_b = pb("ps_b")
        ps_h = [pb("ps_h0"), pb("ps_h1")]
        ps_u = [pb("ps_u0"), pb("ps_u1")]
        ps_c = pb("ps_c")
        ps_y = pb("ps_y")

        ctx_in = sem("ctx_in")
        x_in = [sem(f"x_in{b}") for b in range(B)]
        gamma_in = sem("gamma_in")
        gate_in = sem("gate_in")
        w_in = [sem(f"w_in{s}") for s in range(SLOTS)]
        pool_self = sem("pool_self")
        act_self = sem("act_self")
        dve_self = sem("dve_self")
        ident_ready = sem("ident_ready")
        pick_ready = sem("pick_ready")
        consts_ready = sem("consts_ready")
        gamma_tanh = sem("gamma_tanh")
        gamma_ready = sem("gamma_ready")
        gate_hi = sem("gate_hi")
        gate_ready = sem("gate_ready")
        w_hi = sem("w_hi")
        w_lo = sem("w_lo")
        qk_ready = sem("qk_ready")
        qk_copied = sem("qk_copied")
        sim_ready = sem("sim_ready")
        sim_copied = sem("sim_copied")
        tanh_ready = sem("tanh_ready")
        sig_ready = sem("sig_ready")
        stats1_ready = sem("stats1_ready")
        base_ready = sem("base_ready")
        masked_ready = sem("masked_ready")
        maskT_ready = sem("maskT_ready")
        x1_ready = sem("x1_ready")
        stats2_ready = sem("stats2_ready")
        rs2_ready = sem("rs2_ready")
        z_ready = sem("z_ready")
        zT_ready = sem("zT_ready")
        zhi_ready = sem("zhi_ready")
        zlo_ready = sem("zlo_ready")
        logits_ready = sem("logits_ready")
        lgd_ready = sem("lgd_ready")
        exp_ready = sem("exp_ready")
        comb_ready = sem("comb_ready")
        combT_ready = sem("combT_ready")
        combT_copied = sem("combT_copied")
        h_ready = sem("h_ready")
        u_ready = sem("u_ready")
        silu_ready = sem("silu_ready")
        prod_ready = sem("prod_ready")
        spread_ready = sem("spread_ready")
        gc_ready = sem("gc_ready")
        ghi_ready = sem("ghi_ready")
        glo_ready = sem("glo_ready")
        down_done = sem("down_done")
        fin_ready = sem("fin_ready")
        out_done = sem("out_done")

        block = es.enter_context(nc.Block())

        @block.sync
        def _(sp):
            sp.dma_start(ctx_sb[:, :], ctxT).then_inc(ctx_in, 16)
            sp.dma_start(wqk_sb[:, 0, :], wqT).then_inc(ctx_in, 16)
            sp.dma_start(wqk_sb[:, 1, :], wkT).then_inc(ctx_in, 16)
            sp.dma_start(x_sb[:, 0, :, :], x[0].rearrange("(t p) d -> p t d", p=P)).then_inc(x_in[0], 16)
            sp.dma_start(gamma_sb[:, :], gamma.partition_broadcast(P)).then_inc(gamma_in, 16)
            sp.dma_start(gate_sb[:, :, :], gateT).then_inc(gate_in, 16)
            sp.dma_start(up_raw[:, 0, 0, :, :], ws1t).then_inc(w_in[0], 16)
            sp.dma_start(up_raw[:, 0, 1, :, :], ws3t).then_inc(w_in[0], 16)
            sp.dma_start(dn_raw[:, 0, :], ws2t).then_inc(w_in[0], 16)
            for s in range(1, SLOTS):
                e = 2 * s - 2
                sp.dma_start(up_raw[:, 1 + e:3 + e, 0, :, :], w1t[:, e:e + 2, :, :]).then_inc(w_in[s], 16)
                sp.dma_start(up_raw[:, 1 + e:3 + e, 1, :, :], w3t[:, e:e + 2, :, :]).then_inc(w_in[s], 16)
                sp.dma_start(dn_raw[:, 1 + e:3 + e, :], w2t[:, e:e + 2, :]).then_inc(w_in[s], 16)
            for b in range(1, B):
                sp.dma_start(x_sb[:, b, :, :], x[b].rearrange("(t p) d -> p t d", p=P)).then_inc(x_in[b], 16)
            for b in range(B):
                sp.wait_ge(fin_ready, b + 1)
                sp.dma_start(out[b].rearrange("(t p) d -> p t d", p=P), fin[b][:, :, :]).then_inc(out_done, 16)
            sp.wait_ge(out_done, 16 * B)

        @block.gpsimd
        def _(pool):
            done = [0]

            def link(ins):
                done[0] += 1
                ins.then_inc(pool_self, 1)
                pool.wait_ge(pool_self, done[0])

            def lower_parts(s):
                ps = experts_of(s)
                a, z_ = ps[0], ps[-1] + 1
                pool.wait_ge(w_hi, 2 * s + 1)
                nc.gpsimd.tensor_tensor(up_lo[:, a:z_], up_raw[:, a:z_], up_hi[:, a:z_].bitcast(F32),
                                        ALU.subtract).then_inc(w_lo, 1)
                pool.wait_ge(w_hi, 2 * s + 2)
                nc.gpsimd.tensor_tensor(dn_lo[:, a:z_], dn_raw[:, a:z_], dn_hi[:, a:z_].bitcast(F32),
                                        ALU.subtract).then_inc(w_lo, 1)

            def norm1(b):
                pool.wait_ge(stats1_ready, b + 1)
                link(nc.gpsimd.tensor_scalar(var1[:, :], mv1[:, :, 1], 1e-5, None, ALU.add))
                link(nc.gpsimd.tensor_tensor(rs1[:, :], var1[:, :], minus_half[:, :], ALU.pow))
                if b == 0:
                    pool.wait_ge(gamma_ready, 1)
                link(nc.gpsimd.tensor_scalar(c1[:, :], rs1[:, :], g_rest[:, 0:1], None, ALU.mult))
                nc.gpsimd.tensor_scalar(sc1[:, :], c1[:, :], 1.0, None, ALU.add)
                link(nc.gpsimd.tensor_tensor(mc1[:, :], mv1[:, :, 0], c1[:, :], ALU.mult))
                link(nc.gpsimd.tensor_scalar(bi1[:, :], mc1[:, :], -1.0, None, ALU.mult))
                for t in range(T):
                    last = nc.gpsimd.tensor_scalar(ln1[:, t, :], x_sb[:, b, t, :], sc1[:, t:t + 1],
                                                   bi1[:, t:t + 1], ALU.mult, ALU.add)
                link(last)

            def sigmoid(b):
                pool.wait_ge(tanh_ready, b + 1)
                nc.gpsimd.tensor_scalar(sig[:, :, :], sig[:, :, :], g_quarter[:, 0:1], g_quarter[:, 0:1],
                                        ALU.mult, ALU.add).then_inc(sig_ready, 1)

            def add_masked(b):
                pool.wait_ge(masked_ready, T * (b + 1))
                nc.gpsimd.tensor_tensor(base[:, :, :], ln1[:, :, :], masked[:, :, :],
                                        ALU.add).then_inc(base_ready, 1)

            def norm2(b):
                pool.wait_ge(stats2_ready, b + 1)
                link(nc.gpsimd.tensor_scalar(var2[:, :], mv2[:, :, 1], 1e-5, None, ALU.add))
                nc.gpsimd.tensor_tensor(rs2[:, :], var2[:, :], minus_half[:, :], ALU.pow).then_inc(rs2_ready, 1)

            def exps(b):
                pool.wait_ge(lgd_ready, b + 1)
                nc.gpsimd.tensor_tensor(ex[:, :, :], euler[:, :, :], lgd[:, :, :], ALU.pow).then_inc(exp_ready, 1)

            def low_g(b, s):
                i = SLOTS * b + s
                w = N * len(experts_of(s))
                pool.wait_ge(ghi_ready, i + 1)
                nc.gpsimd.tensor_tensor(g_lo[i % 3][:, :w], gc[i % 2][:, :w], g_hi[i % 3][:, :w].bitcast(F32),
                                        ALU.subtract).then_inc(glo_ready, 1)

            nc.gpsimd.memset(ident[:, :], 0.0).then_inc(ident_ready, 1)
            pool.wait_ge(ident_ready, 1)
            nc.gpsimd.affine_select(out=ident[:, :], in_=ident[:, :], compare_op=ALU.not_equal, fill=1.0, base=0,
                                    pattern=[[-1, P]], channel_multiplier=1).then_inc(ident_ready, 1)
            nc.gpsimd.memset(minus_half[:, :], -0.5)
            nc.gpsimd.memset(euler[:, :, :], 2.718281828459045)
            nc.gpsimd.memset(lgx[:, :, :], LOWEST)
            nc.gpsimd.memset(take[:, :, :], LOWEST).then_inc(consts_ready, 1)
            pool.wait_ge(consts_ready, 1)
            link(nc.gpsimd.memset(pick[:, :, :], 0.0))
            for half in range(2):
                link(nc.gpsimd.affine_select(out=pick[:, :, :], in_=pick[:, :, :], compare_op=ALU.not_equal, fill=1.0,
                                             base=-E * half, pattern=[[-1, E], [0, P]], channel_multiplier=1))
            nc.gpsimd.tensor_copy(pick_r[:, :, :], pick[:, :, :]).then_inc(pick_ready, 1)
            norm1(0)
            lower_parts(0)
            sigmoid(0)
            for s in range(1, SLOTS):
                lower_parts(s)
            add_masked(0)
            norm2(0)
            exps(0)
            for b in range(B):
                low_g(b, 0)
                if b + 1 < B:
                    norm1(b + 1)
                low_g(b, 1)
                if b + 1 < B:
                    sigmoid(b + 1)
                low_g(b, 2)
                low_g(b, 3)
                low_g(b, 4)
                if b + 1 < B:
                    add_masked(b + 1)
                    norm2(b + 1)
                    exps(b + 1)

        @block.scalar
        def _(act):
            nc.scalar.preload_act_table(ACT.Silu)

            def upper_parts(s):
                ps = experts_of(s)
                a, z_ = ps[0], ps[-1] + 1
                act.wait_ge(w_in[s], 48)
                nc.scalar.activation(up_hi[:, a:z_], up_raw[:, a:z_], ACT.Copy).then_inc(w_hi, 1)
                nc.scalar.activation(dn_hi[:, a:z_], dn_raw[:, a:z_], ACT.Copy).then_inc(w_hi, 1)

            def copy_qk(b):
                act.wait_ge(qk_ready, b + 1)
                nc.scalar.activation(qkT[:, :, :], ps_b[0:DC, :].rearrange("p (a n) -> p a n", a=2),
                                     ACT.Copy).then_inc(qk_copied, 1)

            def copy_scores(b):
                act.wait_ge(sim_ready, b + 1)
                v = ps_b[:, :].rearrange("p (t n) -> p t n", t=T)
                if b >= 1:
                    act.wait_ge(masked_ready, T * b)
                nc.scalar.activation(scores[:, :, :], v, ACT.Copy).then_inc(sim_copied, 1)
                nc.scalar.activation(sig[:, :, :], v, ACT.Tanh, scale=SIM_SCALE / 2).then_inc(tanh_ready, 1)

            def high_z(b):
                act.wait_ge(zT_ready, b + 1)
                if b >= 2:
                    act.wait_ge(u_ready, SLOTS * (b - 1))
                nc.scalar.activation(z_hi[b % 2][:, :, :], ps_b[:, :].rearrange("p (k n) -> p k n", k=KD),
                                     ACT.Copy).then_inc(zhi_ready, 1)

            def copy_combT(b):
                act.wait_ge(combT_ready, b + 1)
                if b >= 1:
                    act.wait_ge(spread_ready, 4 * b)
                nc.scalar.activation(combT[:, :], ps_a[0:2 * E, 0:N], ACT.Copy).then_inc(combT_copied, 1)

            def silu(b, s):
                i = SLOTS * b + s
                w = N * len(experts_of(s))
                act.wait_ge(h_ready, i + 1)
                if i >= 2:
                    act.wait_ge(prod_ready, i - 1)
                nc.scalar.activation(sil[i % 2][:, :w], ps_h[i % 2][:, :w], ACT.Silu).then_inc(silu_ready, 1)

            def high_g(b, s):
                i = SLOTS * b + s
                w = N * len(experts_of(s))
                if s == 0:
                    act.wait_ge(prod_ready, i + 1)
                else:
                    act.wait_ge(gc_ready, 4 * b + s)
                if i >= 3:
                    act.wait_ge(down_done, i - 2)
                nc.scalar.activation(g_hi[i % 3][:, :w], gc[i % 2][:, :w], ACT.Copy).then_inc(ghi_ready, 1)

            copy_qk(0)
            copy_scores(0)
            act.wait_ge(gamma_in, 16)
            nc.scalar.activation(g_tanh[:, :], gamma_sb[:, :], ACT.Tanh, scale=0.5).then_inc(gamma_tanh, 1)
            act.wait_ge(gate_in, 16)
            nc.scalar.activation(gate_r[:, :, 0, :], gate_sb[:, :, :], ACT.Copy).then_inc(gate_hi, 1)
            for s in range(SLOTS):
                upper_parts(s)
            high_z(0)
            for b in range(B):
                silu(b, 0)
                high_g(b, 0)
                if b + 1 < B:
                    copy_qk(b + 1)
                silu(b, 1)
                if b + 1 < B:
                    copy_scores(b + 1)
                copy_combT(b)
                high_g(b, 1)
                for s in range(2, SLOTS):
                    silu(b, s)
                    high_g(b, s)
                if b + 1 < B:
                    high_z(b + 1)

        @block.vector
        def _(dve):
            done = [0]

            def link(ins):
                done[0] += 1
                ins.then_inc(dve_self, 1)
                dve.wait_ge(dve_self, done[0])

            def stats(src, st, mv, ready):
                for t in range(T):
                    last = nc.vector.bn_stats(st[:, t, :], src[:, t, :])
                link(last)
                for t in range(T):
                    last = nc.vector.bn_aggr(mv[:, t, :], st[:, t, :])
                last.then_inc(ready, 1)

            def norm1(b):
                dve.wait_ge(x_in[b], 16)
                if b >= 1:
                    dve.wait_ge(base_ready, b)
                stats(x_sb[:, b], st1, mv1, stats1_ready)

            def topk(b, first, last_):
                if first == 0:
                    dve.wait_ge(sim_copied, b + 1)
                for r in range(first, last_):
                    for t in range(T):
                        src = scores if r == 0 else left
                        if r > 0:
                            dve.wait_ge(dve_self, done[0] - T + 1)
                        nc.vector.max(top8[:, t, :], src[:, t, :]).then_inc(dve_self, 1)
                        done[0] += 1
                    if r == ROUNDS - 1:
                        break
                    for t in range(T):
                        src = scores if r == 0 else left
                        dve.wait_ge(dve_self, done[0] - T + 1)
                        nc.vector.match_replace(out=left[:, t, :], in_to_replace=top8[:, t, :],
                                                in_values=src[:, t, :], imm_value=LOWEST).then_inc(dve_self, 1)
                        done[0] += 1

            def mask(b):
                dve.wait_ge(sig_ready, b + 1)
                dve.wait_ge(dve_self, done[0])
                for t in range(T):
                    nc.vector.scalar_tensor_tensor(masked[:, t, :], scores[:, t, :], top8[:, t, KTH:KTH + 1],
                                                   sig[:, t, :], ALU.is_ge, ALU.mult).then_inc(masked_ready, 1)

            def residual1(b):
                dve.wait_ge(maskT_ready, b + 1)
                dve.wait_ge(base_ready, b + 1)
                if b >= 2:
                    dve.wait_ge(fin_ready, b - 1)
                nc.vector.tensor_tensor(x1[b % 2][:, :, :], base[:, :, :],
                                        ps_a[:, :].rearrange("p (t n) -> p t n", t=T), ALU.add).then_inc(x1_ready, 1)
                dve.wait_ge(x1_ready, b + 1)
                stats(x1[b % 2], st2, mv2, stats2_ready)

            def norm2(b):
                dve.wait_ge(rs2_ready, b + 1)
                dve.wait_ge(stats2_ready, b + 1)
                for t in range(T):
                    nc.vector.tensor_scalar(z[:, t, :], x1[b % 2][:, t, :], mv2[:, t, 0:1], rs2[:, t:t + 1],
                                            ALU.subtract, ALU.mult).then_inc(z_ready, 1)

            def low_z(b):
                dve.wait_ge(zhi_ready, b + 1)
                nc.vector.tensor_tensor(z_lo[b % 2][:, :, :], ps_b[:, :].rearrange("p (k n) -> p k n", k=KD),
                                        z_hi[b % 2][:, :, :].bitcast(F32), ALU.subtract).then_inc(zlo_ready, 1)

            def route_a(b):
                dve.wait_ge(logits_ready, b + 1)
                link(nc.vector.tensor_copy(lgp[:, :, :, :],
                                           ps_a[:, 0:T * 2 * E].rearrange("p (t a e) -> p t a e", t=T, a=2)))
                link(nc.vector.tensor_tensor(lgx[:, :, 0:E], lgp[:, :, 0, :], lgp[:, :, 1, :], ALU.add))
                for t in range(T):
                    last = nc.vector.max(lg8[:, t, :], lgx[:, t, 0:E])
                link(last)
                nc.vector.tensor_copy(take[:, :, 0:2], lg8[:, :, 0:2]).then_inc(dve_self, 1)
                done[0] += 1
                if b >= 1:
                    dve.wait_ge(exp_ready, b)
                nc.vector.tensor_tensor(lgd[:, :, :], lgx[:, :, 0:E], lg8[:, :, 0:1].broadcast_to([P, T, E]),
                                        ALU.subtract).then_inc(lgd_ready, 1)
                dve.wait_ge(dve_self, done[0])
                for t in range(T):
                    last = nc.vector.match_replace(out=rest[:, t, :], in_to_replace=take[:, t, :],
                                                   in_values=lgx[:, t, :], imm_value=LOWEST)
                link(last)
                link(nc.vector.tensor_tensor(chosen[:, :, :], lgx[:, :, 0:E], rest[:, :, 0:E], ALU.not_equal))

            def route_b(b):
                dve.wait_ge(exp_ready, b + 1)
                nc.vector.tensor_reduce(exs[:, :], ex[:, :, :], axis=mybir.AxisListType.X, op=ALU.add)\
                    .then_inc(dve_self, 1)
                done[0] += 1
                nc.vector.tensor_tensor(exc[:, :, :], ex[:, :, :], chosen[:, :, :], ALU.mult)
                dve.wait_ge(dve_self, done[0])
                link(nc.vector.reciprocal(exr[:, :], exs[:, :]))
                link(nc.vector.tensor_tensor(comb[:, :, :], exc[:, :, :],
                                             exr[:, :].unsqueeze(2).broadcast_to([P, T, E]), ALU.mult))
                link(nc.vector.tensor_copy(comb_r[:, :, 0, :], comb[:, :, :]))
                nc.vector.tensor_tensor(comb_r[:, :, 1, :], comb[:, :, :], comb_r[:, :, 0, :].bitcast(F32),
                                        ALU.subtract).then_inc(comb_ready, 1)

            def gate_values(b, s):
                i = SLOTS * b + s
                w = N * len(experts_of(s))
                dve.wait_ge(silu_ready, i + 1)
                dve.wait_ge(u_ready, i + 1)
                if i >= 2:
                    dve.wait_ge(glo_ready, i - 1)
                if s == 0:
                    nc.vector.tensor_tensor(gc[i % 2][:, :w], sil[i % 2][:, :w], ps_u[i % 2][:, :w],
                                            ALU.mult).then_inc(prod_ready, 1)
                else:
                    nc.vector.tensor_tensor(prod[:, :w], sil[i % 2][:, :w], ps_u[i % 2][:, :w],
                                            ALU.mult).then_inc(prod_ready, 1)
                    dve.wait_ge(prod_ready, i + 1)
                    dve.wait_ge(spread_ready, 4 * b + s)
                    nc.vector.tensor_tensor(gc[i % 2][:, :w], prod[:, :w], ps_c[:, :w],
                                            ALU.mult).then_inc(gc_ready, 1)

            def residual2(b):
                dve.wait_ge(down_done, SLOTS * (b + 1))
                nc.vector.tensor_tensor(fin[b][:, :, :], x1[b % 2][:, :, :],
                                        ps_y[:, :].rearrange("p (t d) -> p t d", t=T), ALU.add).then_inc(fin_ready, 1)

            norm1(0)
            dve.wait_ge(gamma_tanh, 1)
            nc.vector.tensor_scalar(g_rest[:, :], g_tanh[:, :], -0.5, 0.5, ALU.mult, ALU.add)
            nc.vector.tensor_scalar(g_quarter[:, :], g_tanh[:, :], 0.125, 0.125, ALU.mult, ALU.add)\
                .then_inc(gamma_ready, 1)
            topk(0, 0, ROUNDS)
            mask(0)
            dve.wait_ge(gate_hi, 1)
            nc.vector.tensor_tensor(gate_r[:, :, 1, :], gate_sb[:, :, :], gate_r[:, :, 0, :].bitcast(F32),
                                    ALU.subtract).then_inc(gate_ready, 1)
            residual1(0)
            norm2(0)
            low_z(0)
            dve.wait_ge(consts_ready, 1)
            route_a(0)
            for b in range(B):
                gate_values(b, 0)
                route_b(b)
                if b + 1 < B:
                    norm1(b + 1)
                gate_values(b, 1)
                if b + 1 < B:
                    topk(b + 1, 0, 3)
                gate_values(b, 2)
                if b + 1 < B:
                    topk(b + 1, 3, 6)
                gate_values(b, 3)
                if b + 1 < B:
                    topk(b + 1, 6, 9)
                gate_values(b, 4)
                if b + 1 < B:
                    topk(b + 1, 9, ROUNDS)
                    mask(b + 1)
                    residual1(b + 1)
                    norm2(b + 1)
                    low_z(b + 1)
                    residual2(b)
                    route_a(b + 1)
                else:
                    residual2(b)

        @block.tensor
        def _(pe):
            def project(b):
                if b == 0:
                    pe.wait_ge(ctx_in, 48)
                else:
                    pe.wait_ge(zlo_ready, b)
                for a in range(2):
                    last = nc.tensor.matmul(ps_b[0:DC, a * N:(a + 1) * N], wqk_sb[:, a, :],
                                            ctx_sb[:, b * N:(b + 1) * N], start=True, stop=True)
                last.then_inc(qk_ready, 1)

            def similar(b):
                pe.wait_ge(qk_copied, b + 1)
                for t in range(T):
                    last = nc.tensor.matmul(ps_b[:, t * N:(t + 1) * N], qkT[:, 0, t * P:(t + 1) * P], qkT[:, 1, :],
                                            start=True, stop=True)
                last.then_inc(sim_ready, 1)

            def transpose_masked(b):
                if b == 0:
                    pe.wait_ge(ident_ready, 2)
                else:
                    pe.wait_ge(combT_copied, b)
                for t in range(T):
                    pe.wait_ge(masked_ready, T * b + t + 1)
                    for j in range(T):
                        last = nc.tensor.transpose(ps_a[:, j * N + t * P:j * N + (t + 1) * P],
                                                   masked[:, t, j * P:(j + 1) * P], ident[:, :])
                last.then_inc(maskT_ready, 1)

            def transpose_z(b):
                pe.wait_ge(tanh_ready, b + 1)
                for t in range(T):
                    pe.wait_ge(z_ready, T * b + t + 1)
                    for k in range(KD):
                        last = nc.tensor.transpose(ps_b[:, k * N + t * P:k * N + (t + 1) * P],
                                                   z[:, t, k * P:(k + 1) * P], ident[:, :])
                last.then_inc(zT_ready, 1)

            def logits(b):
                pe.wait_ge(zhi_ready, b + 1)
                if b == 0:
                    pe.wait_ge(gate_ready, 1)
                pe.wait_ge(zlo_ready, b + 1)
                pe.wait_ge(x1_ready, b + 1)
                for t in range(T):
                    n = 0
                    for zz in (z_hi, z_lo):
                        for k in range(KD):
                            last = nc.tensor.matmul(ps_a[:, t * 2 * E:(t + 1) * 2 * E],
                                                    zz[b % 2][:, k, t * P:(t + 1) * P],
                                                    gate_r[:, k, :, :].rearrange("p a e -> p (a e)"),
                                                    start=(n == 0), stop=(n == 2 * KD - 1))
                            n += 1
                last.then_inc(logits_ready, 1)

            def transpose_comb(b):
                pe.wait_ge(comb_ready, b + 1)
                for t in range(T):
                    last = nc.tensor.transpose(ps_a[0:2 * E, t * P:(t + 1) * P],
                                               comb_r[:, t, :, :].rearrange("p a e -> p (a e)").bitcast(F32),
                                               ident[:, :])
                last.then_inc(combT_ready, 1)

            def up(b, s):
                i = SLOTS * b + s
                if b == 0:
                    pe.wait_ge(w_hi, 2 * s + 2)
                    pe.wait_ge(w_lo, 2 * s + 2)
                if i >= 2:
                    pe.wait_ge(silu_ready, i - 1)
                    pe.wait_ge(prod_ready, i - 1)
                for a, (bank, ready) in enumerate(((ps_h, h_ready), (ps_u, u_ready))):
                    for n, e in enumerate(experts_of(s)):
                        dst = bank[i % 2][:, n * N:(n + 1) * N]
                        m = 0
                        for w, zz in ((up_hi, z_hi), (up_lo, z_hi), (up_hi, z_lo)):
                            for k in range(KD):
                                last = nc.tensor.matmul(dst, w[:, e, a, k, :], zz[b % 2][:, k, :],
                                                        start=(m == 0), stop=(m == 3 * KD - 1))
                                m += 1
                    last.then_inc(ready, 1)

            def spread(b, s):
                if s == 1:
                    pe.wait_ge(combT_copied, b + 1)
                if b == 0 and s == 1:
                    pe.wait_ge(pick_ready, 1)
                if b > 0 or s > 1:
                    pe.wait_ge(gc_ready, 4 * b + s - 1)
                for n in range(2):
                    last = nc.tensor.matmul(ps_c[:, n * N:(n + 1) * N], pick_r[:, 2 * s - 2 + n, :], combT[:, :],
                                            start=True, stop=True)
                last.then_inc(spread_ready, 1)

            def down(b, s):
                i = SLOTS * b + s
                if s == 0 and b >= 1:
                    pe.wait_ge(fin_ready, b)
                pe.wait_ge(ghi_ready, i + 1)
                pe.wait_ge(glo_ready, i + 1)
                for n, e in enumerate(experts_of(s)):
                    for t in range(T):
                        tok = slice(n * N + t * P, n * N + (t + 1) * P)
                        for m, (g, w) in enumerate(((g_hi, dn_hi), (g_hi, dn_lo), (g_lo, dn_hi))):
                            last = nc.tensor.matmul(ps_y[:, t * D:(t + 1) * D], g[i % 3][:, tok], w[:, e, :],
                                                    start=(s == 0 and t == 0 and m == 0),
                                                    stop=(s == SLOTS - 1 and n == 1 and m == 2),
                                                    skip_group_check=True)
                last.then_inc(down_done, 1)

            project(0)
            similar(0)
            transpose_masked(0)
            transpose_z(0)
            logits(0)
            for b in range(B):
                up(b, 0)
                if b + 1 < B:
                    project(b + 1)
                up(b, 1)
                if b + 1 < B:
                    similar(b + 1)
                transpose_comb(b)
                spread(b, 1)
                for s in range(2, SLOTS):
                    up(b, s)
                    down(b, s - 2)
                    spread(b, s)
                if b + 1 < B:
                    transpose_masked(b + 1)
                down(b, SLOTS - 2)
                if b + 1 < B:
                    transpose_z(b + 1)
                down(b, SLOTS - 1)
                if b + 1 < B:
                    logits(b + 1)


def kernel(**inputs):
    import numpy as np
    import concourse.bacc as bacc
    from concourse.bass_utils import run_bass_kernel_spmd

    f = {k: np.asarray(v) for k, v in inputs.items()}

    def up_layout(w):
        e = w.shape[0]
        return w.transpose(2, 0, 1).reshape(KD, P, e, INTER).transpose(1, 2, 0, 3)

    arrays = {
        "x": f["x"],
        "ctxT": f["ctx_512"].transpose(2, 0, 1).reshape(DC, B * N),
        "wqT": f["L0_xattn_Wq"].T,
        "wkT": f["L0_xattn_Wk"].T,
        "gamma": f["L0_xattn_gamma_raw"].reshape(1),
        "gateT": f["L0_ffn_gate_w"].T.reshape(KD, P, E).transpose(1, 0, 2),
        "w1t": up_layout(f["L0_ffn_w1"]),
        "w3t": up_layout(f["L0_ffn_w3"]),
        "w2t": f["L0_ffn_w2"].transpose(2, 0, 1),
        "ws1t": up_layout(f["L0_ffn_ws1"][None])[:, 0],
        "ws3t": up_layout(f["L0_ffn_ws3"][None])[:, 0],
        "ws2t": f["L0_ffn_ws2"].T,
    }
    arrays = {f"in_{k}": np.ascontiguousarray(v) for k, v in arrays.items()}
    nc = bacc.Bacc("TRN2", target_bir_lowering=False, num_devices=1)
    args = [nc.dram_tensor(k, v.shape, mybir.dt.from_np(v.dtype), kind="ExternalInput").ap()
            for k, v in arrays.items()]
    args.append(nc.dram_tensor("out_x", (B, N, D), F32, kind="ExternalOutput").ap())
    attention_ffn(nc, *args)
    r = run_bass_kernel_spmd(nc, [arrays], core_ids=[0])
    return r.results[0]["out_x"]
```

```python
import concourse.bass as bass
from concourse import mybir
from contextlib import ExitStack

F32 = mybir.dt.float32
F32R = mybir.dt.float32r
ALU = mybir.AluOpType
ACT = mybir.ActivationFunctionType

P = 128
B = 4
N = 256
D = 256
DC = 64
HEADS = 4
T = N // P
KD = D // P
E = 8
INTER = 128
TOPK = int(N * 0.3)
SIM_SCALE = 1.0 / (float(DC // HEADS) ** 0.5 * HEADS)
LOWEST = -3.0e38
ROUNDS = (TOPK + 7) // 8
KTH = (TOPK - 1) % 8
WINDOW = 24
AIM = TOPK - WINDOW // 2 - 1
FIRST_PIVOT = 0.6
DENSITY = 118.0
FILL = 6
SLOTS = 1 + E // 2


def experts_of(slot):
    return [0] if slot == 0 else [2 * slot - 1, 2 * slot]


def attention_ffn(nc, x, ctxT, wqkT, gamma, gateT, w1t, w3t, w2t, ws1t, ws3t, ws2t, out):
    es = ExitStack()
    with es:
        def sb(name, shape, dt=F32):
            return es.enter_context(nc.sbuf_tensor(name, shape, dt))

        def pb(name):
            return es.enter_context(nc.psum_tensor(name, [P, 512], F32))

        def sem(name):
            return es.enter_context(nc.semaphore(name))

        x_sb = sb("x_sb", [P, B, T, D])
        ctx_sb = sb("ctx_sb", [DC, B * N])
        wqk_sb = sb("wqk_sb", [DC, 2, DC])
        gamma_sb = sb("gamma_sb", [P, 1])
        gate_sb = sb("gate_sb", [P, KD, E])
        gate_r = sb("gate_r", [P, KD, 2, E], F32R)
        up_raw = sb("up_raw", [P, 1 + E, 2, KD, INTER])
        up_hi = sb("up_hi", [P, 1 + E, 2, KD, INTER], F32R)
        up_lo = sb("up_lo", [P, 1 + E, 2, KD, INTER], F32R)
        dn_raw = sb("dn_raw", [P, 1 + E, D])
        dn_hi = sb("dn_hi", [P, 1 + E, D], F32R)
        dn_lo = sb("dn_lo", [P, 1 + E, D], F32R)
        ident = sb("ident", [P, P])
        pick = sb("pick", [2 * E, E, P])
        pick_r = sb("pick_r", [2 * E, E, P], F32R)
        minus_half = sb("minus_half", [P, T])
        plus_half = sb("plus_half", [P, T])
        ones = sb("ones", [P, 1])
        above = sb("above", [P, T, WINDOW])
        euler = sb("euler", [P, T, E])
        g_tanh = sb("g_tanh", [P, 1])
        g_rest = sb("g_rest", [P, 1])
        g_quarter = sb("g_quarter", [P, 1])

        qkT = sb("qkT", [DC, 2, N])
        scores = [sb(f"scores{i}", [P, T, N]) for i in range(2)]
        left = sb("left", [P, T, N])
        top8 = sb("top8", [P, T, 8])
        st0 = sb("st0", [P, T, 6])
        mv0 = sb("mv0", [P, T, 2])
        dev = sb("dev", [P, T])
        step = sb("step", [P, T])
        offset = sb("offset", [P, T])
        neg_pivot = sb("neg_pivot", [P, T])
        sides = [sb(f"sides{t}", [P, N]) for t in range(T)]
        balance = sb("balance", [P, T])
        excess = sb("excess", [P, T])
        pivot = sb("pivot", [P, T])
        delta = sb("delta", [P, T])
        count = sb("count", [P, T])
        over = sb("over", [P, T, N])
        near = sb("near", [P, T, WINDOW])
        place = sb("place", [P, T, WINDOW])
        hit = sb("hit", [P, 1])
        hits = sb("hits", [1, 1], mybir.dt.int32)
        kth_pick = sb("kth_pick", [P, T, WINDOW])
        kth = sb("kth", [P, T])
        sig = [sb(f"sig{i}", [P, T, N]) for i in range(2)]
        masked = sb("masked", [P, T, N])
        st1 = [sb(f"st1_{i}", [P, T, 6]) for i in range(2)]
        mv1 = [sb(f"mv1_{i}", [P, T, 2]) for i in range(2)]
        var1 = sb("var1", [P, T])
        rs1 = sb("rs1", [P, T])
        c1 = sb("c1", [P, T])
        sc1 = sb("sc1", [P, T])
        mc1 = sb("mc1", [P, T])
        bi1 = sb("bi1", [P, T])
        ln1 = sb("ln1", [P, T, N])
        base = sb("base", [P, T, N])
        x1 = [sb(f"x1_{i}", [P, T, D]) for i in range(2)]
        st2 = sb("st2", [P, T, 6])
        mv2 = sb("mv2", [P, T, 2])
        var2 = sb("var2", [P, T])
        rs2 = sb("rs2", [P, T])
        z = sb("z", [P, T, D])
        z_hi = [sb(f"z_hi{i}", [P, KD, N], F32R) for i in range(2)]
        z_lo = [sb(f"z_lo{i}", [P, KD, N], F32R) for i in range(2)]

        lgx = sb("lgx", [P, T, E + FILL])
        lgT = sb("lgT", [2 * E, N])
        lgp = sb("lgp", [P, T, 2, E])
        lg8 = sb("lg8", [P, T, 8])
        take = sb("take", [P, T, 8])
        rest = sb("rest", [P, T, E + FILL])
        lgd = sb("lgd", [P, T, E])
        ex = sb("ex", [P, T, E])
        exs = sb("exs", [P, T])
        exr = sb("exr", [P, T])
        chosen = sb("chosen", [P, T, E])
        exc = sb("exc", [P, T, E])
        comb = sb("comb", [P, T, E])
        comb_r = sb("comb_r", [P, T, 2, E], F32R)
        combT = sb("combT", [2 * E, N], F32R)

        sil = [sb(f"sil{i}", [P, 512]) for i in range(2)]
        prod = [sb(f"prod{i}", [P, 512]) for i in range(2)]
        gc = [sb(f"gc{i}", [P, 512]) for i in range(2)]
        g_hi = [sb(f"g_hi{i}", [P, 512], F32R) for i in range(3)]
        g_lo = [sb(f"g_lo{i}", [P, 512], F32R) for i in range(3)]
        fin = [sb(f"fin{b}", [P, T, D]) for b in range(B)]

        ps_a = pb("ps_a")
        ps_b = pb("ps_b")
        ps_h = [pb("ps_h0"), pb("ps_h1")]
        ps_u = [pb("ps_u0"), pb("ps_u1")]
        ps_c = pb("ps_c")
        ps_y = pb("ps_y")

        ctx0_in = sem("ctx0_in")
        ctx_in = sem("ctx_in")
        x_in = [sem(f"x_in{b}") for b in range(B)]
        gamma_in = sem("gamma_in")
        gate_in = sem("gate_in")
        w_in = [sem(f"w_in{s}") for s in range(SLOTS)]
        pool_self = sem("pool_self")
        act_self = sem("act_self")
        dve_self = sem("dve_self")
        ident_ready = sem("ident_ready")
        pick_ready = sem("pick_ready")
        pick_rounded = sem("pick_rounded")
        consts_ready = sem("consts_ready")
        above_ready = sem("above_ready")
        gamma_tanh = sem("gamma_tanh")
        gamma_ready = sem("gamma_ready")
        gate_hi = sem("gate_hi")
        gate_ready = sem("gate_ready")
        w_hi = sem("w_hi")
        up_lo0_ready = sem("up_lo0_ready")
        dn_lo0_ready = sem("dn_lo0_ready")
        up_lo_ready = sem("up_lo_ready")
        dn_lo_ready = sem("dn_lo_ready")
        qk_ready = sem("qk_ready")
        qk_copied = sem("qk_copied")
        sim_ready = sem("sim_ready")
        sim_copied = sem("sim_copied")
        tanh_ready = sem("tanh_ready")
        sig_ready = sem("sig_ready")
        stats0_ready = sem("stats0_ready")
        pivot0_ready = sem("pivot0_ready")
        balance_ready = sem("balance_ready")
        pivot_ready = sem("pivot_ready")
        hit_ready = sem("hit_ready")
        hits_ready = sem("hits_ready")
        hits_taken = sem("hits_taken")
        fallback = [sem(f"fallback{b}") for b in range(B)]
        lgT_ready = sem("lgT_ready")
        lgT_copied = sem("lgT_copied")
        stats1_ready = sem("stats1_ready")
        norm1_done = sem("norm1_done")
        base_ready = sem("base_ready")
        masked_ready = sem("masked_ready")
        maskT_ready = sem("maskT_ready")
        x1_ready = sem("x1_ready")
        stats2_ready = sem("stats2_ready")
        rs2_ready = sem("rs2_ready")
        z_ready = sem("z_ready")
        zT_ready = sem("zT_ready")
        zhi_ready = sem("zhi_ready")
        zlo_ready = sem("zlo_ready")
        logits_ready = sem("logits_ready")
        lgd_ready = sem("lgd_ready")
        exp_ready = sem("exp_ready")
        comb_ready = sem("comb_ready")
        combT_ready = sem("combT_ready")
        combT_copied = sem("combT_copied")
        h_ready = sem("h_ready")
        u_ready = sem("u_ready")
        silu_ready = sem("silu_ready")
        prod_ready = sem("prod_ready")
        spread_ready = sem("spread_ready")
        gc_ready = sem("gc_ready")
        ghi_ready = sem("ghi_ready")
        glo_ready = sem("glo_ready")
        glo_last = sem("glo_last")
        down_done = sem("down_done")
        fin_ready = sem("fin_ready")
        out_done = sem("out_done")

        block = es.enter_context(nc.Block())

        @block.sync
        def _(sp):
            sp.dma_start(wqk_sb[:, :, :], wqkT).then_inc(ctx0_in, 16)
            sp.dma_start(ctx_sb[:, 0:N], ctxT[:, 0:N]).then_inc(ctx0_in, 16)
            sp.dma_start(x_sb[:, 0, :, :], x[0].rearrange("(t p) d -> p t d", p=P)).then_inc(x_in[0], 16)
            sp.dma_start(x_sb[:, 1, :, :], x[1].rearrange("(t p) d -> p t d", p=P)).then_inc(x_in[1], 16)
            sp.dma_start(up_raw[:, 0, 0, :, :], ws1t).then_inc(w_in[0], 16)
            sp.dma_start(up_raw[:, 0, 1, :, :], ws3t).then_inc(w_in[0], 16)
            sp.dma_start(dn_raw[:, 0, :], ws2t).then_inc(w_in[0], 16)
            for s in range(1, SLOTS):
                e = 2 * s - 2
                sp.dma_start(up_raw[:, 1 + e:3 + e, 0, :, :], w1t[:, e:e + 2, :, :]).then_inc(w_in[s], 16)
                sp.dma_start(up_raw[:, 1 + e:3 + e, 1, :, :], w3t[:, e:e + 2, :, :]).then_inc(w_in[s], 16)
                sp.dma_start(dn_raw[:, 1 + e:3 + e, :], w2t[:, e:e + 2, :]).then_inc(w_in[s], 16)
                if s == 1:
                    sp.dma_start(ctx_sb[:, N:], ctxT[:, N:]).then_inc(ctx_in, 16)
            for b in range(2, B):
                sp.dma_start(x_sb[:, b, :, :], x[b].rearrange("(t p) d -> p t d", p=P)).then_inc(x_in[b], 16)
            for b in range(B):
                sp.wait_ge(fin_ready, b + 1)
                sp.dma_start(out[b].rearrange("(t p) d -> p t d", p=P), fin[b][:, :, :]).then_inc(out_done, 16)
            sp.wait_ge(out_done, 16 * B)

        @block.gpsimd
        def _(pool):
            done = [0]

            def link(ins):
                done[0] += 1
                ins.then_inc(pool_self, 1)
                pool.wait_ge(pool_self, done[0])

            def lower_up(s):
                a, z_ = 2 * s - 1, 2 * s + 1
                pool.wait_ge(w_hi, 2 * s + 1)
                nc.gpsimd.tensor_tensor(up_lo[:, a:z_], up_raw[:, a:z_], up_hi[:, a:z_].bitcast(F32),
                                        ALU.subtract).then_inc(up_lo_ready, 1)

            def lower_down(s):
                a, z_ = 2 * s - 1, 2 * s + 1
                pool.wait_ge(w_hi, 2 * s + 2)
                nc.gpsimd.tensor_tensor(dn_lo[:, a:z_], dn_raw[:, a:z_], dn_hi[:, a:z_].bitcast(F32),
                                        ALU.subtract).then_inc(dn_lo_ready, 1)

            def norm1(b):
                pool.wait_ge(stats1_ready, b + 1)
                link(nc.gpsimd.tensor_scalar(var1[:, :], mv1[b % 2][:, :, 1], 1e-5, None, ALU.add))
                link(nc.gpsimd.tensor_tensor(rs1[:, :], var1[:, :], minus_half[:, :], ALU.pow))
                if b == 0:
                    pool.wait_ge(gamma_ready, 1)
                link(nc.gpsimd.tensor_scalar(c1[:, :], rs1[:, :], g_rest[:, 0:1], None, ALU.mult))
                nc.gpsimd.tensor_scalar(sc1[:, :], c1[:, :], 1.0, None, ALU.add)
                link(nc.gpsimd.tensor_tensor(mc1[:, :], mv1[b % 2][:, :, 0], c1[:, :], ALU.mult))
                link(nc.gpsimd.tensor_scalar(bi1[:, :], mc1[:, :], -1.0, None, ALU.mult))
                for t in range(T):
                    last = nc.gpsimd.tensor_scalar(ln1[:, t, :], x_sb[:, b, t, :], sc1[:, t:t + 1],
                                                   bi1[:, t:t + 1], ALU.mult, ALU.add)
                last.then_inc(norm1_done, 1)

            def first_pivot(b):
                pool.wait_ge(stats0_ready, b + 1)
                link(nc.gpsimd.tensor_tensor(dev[:, :], mv0[:, :, 1], plus_half[:, :], ALU.pow))
                nc.gpsimd.tensor_scalar(step[:, :], dev[:, :], 0.5 / DENSITY, None, ALU.mult)
                link(nc.gpsimd.tensor_scalar(offset[:, :], dev[:, :], -FIRST_PIVOT, None, ALU.mult))
                nc.gpsimd.tensor_tensor(neg_pivot[:, :], offset[:, :], mv0[:, :, 0], ALU.subtract)\
                    .then_inc(pivot0_ready, 1)

            def second_pivot(b):
                pool.wait_ge(balance_ready, b + 1)
                link(nc.gpsimd.tensor_scalar(excess[:, :], balance[:, :], float(N - 2 * AIM), None, ALU.add))
                link(nc.gpsimd.tensor_tensor(delta[:, :], excess[:, :], step[:, :], ALU.mult))
                nc.gpsimd.tensor_tensor(pivot[:, :], delta[:, :], neg_pivot[:, :], ALU.subtract)\
                    .then_inc(pivot_ready, 1)

            def sigmoid(b):
                pool.wait_ge(tanh_ready, b + 1)
                nc.gpsimd.tensor_scalar(sig[b % 2][:, :, :], sig[b % 2][:, :, :], g_quarter[:, 0:1], g_quarter[:, 0:1],
                                        ALU.mult, ALU.add).then_inc(sig_ready, 1)

            def add_masked(b):
                pool.wait_ge(norm1_done, b + 1)
                pool.wait_ge(masked_ready, T * (b + 1))
                nc.gpsimd.tensor_tensor(base[:, :, :], ln1[:, :, :], masked[:, :, :],
                                        ALU.add).then_inc(base_ready, 1)

            def norm2(b):
                pool.wait_ge(stats2_ready, b + 1)
                link(nc.gpsimd.tensor_scalar(var2[:, :], mv2[:, :, 1], 1e-5, None, ALU.add))
                nc.gpsimd.tensor_tensor(rs2[:, :], var2[:, :], minus_half[:, :], ALU.pow).then_inc(rs2_ready, 1)

            def exps(b):
                pool.wait_ge(lgd_ready, b + 1)
                nc.gpsimd.tensor_tensor(ex[:, :, :], euler[:, :, :], lgd[:, :, :], ALU.pow).then_inc(exp_ready, 1)

            def low_g(b, s):
                i = SLOTS * b + s
                w = N * len(experts_of(s))
                pool.wait_ge(ghi_ready, i + 1)
                nc.gpsimd.tensor_tensor(g_lo[i % 3][:, :w], gc[i % 2][:, :w], g_hi[i % 3][:, :w].bitcast(F32),
                                        ALU.subtract).then_inc(glo_ready, 1)

            nc.gpsimd.memset(plus_half[:, :], 0.5)
            nc.gpsimd.memset(minus_half[:, :], -0.5)
            nc.gpsimd.memset(ident[:, :], 0.0).then_inc(ident_ready, 1)
            pool.wait_ge(ident_ready, 1)
            nc.gpsimd.affine_select(out=ident[:, :], in_=ident[:, :], compare_op=ALU.not_equal, fill=1.0, base=0,
                                    pattern=[[-1, P]], channel_multiplier=1).then_inc(ident_ready, 1)
            nc.gpsimd.memset(ones[:, :], 1.0)
            nc.gpsimd.iota(above[:, :, :], pattern=[[0, T], [-1, WINDOW]], base=TOPK - 1, channel_multiplier=0,
                           allow_small_or_imprecise_dtypes=True).then_inc(above_ready, 1)
            nc.gpsimd.memset(euler[:, :, :], 2.718281828459045)
            nc.gpsimd.memset(lgx[:, :, :], LOWEST)
            nc.gpsimd.memset(take[:, :, :], LOWEST).then_inc(consts_ready, 1)
            link(nc.gpsimd.memset(pick[:, :, :], 0.0))
            for half in range(2):
                last = nc.gpsimd.affine_select(out=pick[:, :, :], in_=pick[:, :, :], compare_op=ALU.not_equal,
                                               fill=1.0, base=-E * half, pattern=[[-1, E], [0, P]],
                                               channel_multiplier=1)
                if half == 0:
                    link(last)
            last.then_inc(pick_ready, 1)
            first_pivot(0)
            second_pivot(0)
            norm1(0)
            lower_up(1)
            sigmoid(0)
            lower_up(2)
            add_masked(0)
            first_pivot(1)
            norm2(0)
            second_pivot(1)
            lower_up(3)
            lower_down(1)
            for b in range(B):
                if b + 1 < B:
                    sigmoid(b + 1)
                if b == 0:
                    lower_up(4)
                if b >= 1:
                    low_g(b - 1, 4)
                exps(b)
                if b == 0:
                    norm1(1)
                low_g(b, 0)
                if b + 1 < B:
                    add_masked(b + 1)
                if b == 0:
                    lower_down(2)
                low_g(b, 1)
                if b + 1 < B:
                    norm2(b + 1)
                low_g(b, 2)
                if b + 2 < B:
                    first_pivot(b + 2)
                low_g(b, 3)
                if b == 0:
                    lower_down(3)
                if b + 2 < B:
                    second_pivot(b + 2)
                    norm1(b + 2)
                if b == 0:
                    lower_down(4)
        @block.scalar
        def _(act):
            nc.scalar.preload_act_table(ACT.Silu)
            act.dma_start(gamma_sb[:, :], gamma.partition_broadcast(P)).then_inc(gamma_in, 16)
            act.dma_start(gate_sb[:, :, :], gateT).then_inc(gate_in, 16)

            def upper_parts(s):
                ps = experts_of(s)
                a, z_ = ps[0], ps[-1] + 1
                act.wait_ge(w_in[s], 48)
                nc.scalar.activation(up_hi[:, a:z_], up_raw[:, a:z_], ACT.Copy).then_inc(w_hi, 1)
                nc.scalar.activation(dn_hi[:, a:z_], dn_raw[:, a:z_], ACT.Copy).then_inc(w_hi, 1)

            def copy_qk(b):
                act.wait_ge(qk_ready, b + 1)
                for a in range(2):
                    nc.scalar.activation(qkT[:, a, :], ps_b[a * DC:(a + 1) * DC, 0:N], ACT.Copy)\
                        .then_inc(qk_copied, 1)

            def copy_scores(b):
                v = ps_b[:, :].rearrange("p (t n) -> p t n", t=T)
                if b >= 2:
                    act.wait_ge(masked_ready, T * (b - 1))
                for t in range(T):
                    act.wait_ge(sim_ready, b + 1)
                    nc.scalar.activation(scores[b % 2][:, t, :], v[:, t, :], ACT.Copy).then_inc(sim_copied, 1)
                nc.scalar.activation(sig[b % 2][:, :, :], v, ACT.Tanh, scale=SIM_SCALE / 2).then_inc(tanh_ready, 1)

            def balance_scores(b):
                act.wait_ge(pivot0_ready, b + 1)
                for t in range(T):
                    last = nc.scalar.activation(sides[t][:, :], scores[b % 2][:, t, :], ACT.Sign,
                                                bias=neg_pivot[:, t:t + 1], accum_out=balance[:, t:t + 1])
                last.then_inc(balance_ready, 1)

            def high_z(b):
                act.wait_ge(zT_ready, b + 1)
                if b >= 2:
                    act.wait_ge(u_ready, SLOTS * (b - 1))
                nc.scalar.activation(z_hi[b % 2][:, :, :], ps_b[:, :].rearrange("p (k n) -> p k n", k=KD),
                                     ACT.Copy).then_inc(zhi_ready, 1)

            def copy_logits(b):
                act.wait_ge(lgT_ready, b + 1)
                nc.scalar.activation(lgT[:, :], ps_a[0:2 * E, 0:N], ACT.Copy).then_inc(lgT_copied, 1)

            def copy_combT(b):
                act.wait_ge(combT_ready, b + 1)
                if b >= 1:
                    act.wait_ge(spread_ready, 4 * b)
                nc.scalar.activation(combT[:, :], ps_a[0:2 * E, 0:N], ACT.Copy).then_inc(combT_copied, 1)

            def silu(b, s):
                i = SLOTS * b + s
                w = N * len(experts_of(s))
                act.wait_ge(h_ready, i + 1)
                if i >= 2:
                    act.wait_ge(prod_ready, i - 1)
                nc.scalar.activation(sil[i % 2][:, :w], ps_h[i % 2][:, :w], ACT.Silu).then_inc(silu_ready, 1)

            def high_g(b, s):
                i = SLOTS * b + s
                w = N * len(experts_of(s))
                if s == 0:
                    act.wait_ge(prod_ready, i + 1)
                else:
                    act.wait_ge(gc_ready, 4 * b + s)
                if i >= 3:
                    act.wait_ge(down_done, i - 2)
                nc.scalar.activation(g_hi[i % 3][:, :w], gc[i % 2][:, :w], ACT.Copy).then_inc(ghi_ready, 1)

            def tanh_gamma():
                act.wait_ge(gamma_in, 16)
                nc.scalar.activation(g_tanh[:, :], gamma_sb[:, :], ACT.Tanh, scale=0.5).then_inc(gamma_tanh, 1)

            def upper_gate():
                act.wait_ge(gate_in, 16)
                nc.scalar.activation(gate_r[:, :, 0, :], gate_sb[:, :, :], ACT.Copy).then_inc(gate_hi, 1)

            def round_pick():
                act.wait_ge(pick_ready, 1)
                nc.scalar.activation(pick_r[:, :, :], pick[:, :, :], ACT.Copy).then_inc(pick_rounded, 1)

            upper_gate()
            tanh_gamma()
            copy_qk(0)
            copy_scores(0)
            upper_parts(0)
            copy_qk(1)
            balance_scores(0)
            upper_parts(1)
            copy_scores(1)
            round_pick()
            upper_parts(2)
            upper_parts(3)
            upper_parts(4)
            balance_scores(1)
            high_z(0)
            silu(0, 0)
            copy_logits(0)
            copy_qk(2)
            high_g(0, 0)
            silu(0, 1)
            silu(0, 2)
            silu(0, 3)
            copy_combT(0)
            for b in range(B):
                high_g(b, 1)
                if b + 2 < B:
                    copy_scores(b + 2)
                high_g(b, 2)
                silu(b, 4)
                if b + 1 < B:
                    high_z(b + 1)
                high_g(b, 3)
                if b + 2 < B:
                    balance_scores(b + 2)
                if b + 1 < B:
                    copy_logits(b + 1)
                    silu(b + 1, 0)
                high_g(b, 4)
                if b + 3 < B:
                    copy_qk(b + 3)
                if b + 1 < B:
                    silu(b + 1, 1)
                    high_g(b + 1, 0)
                    silu(b + 1, 2)
                    silu(b + 1, 3)
                    copy_combT(b + 1)
        @block.vector
        def _(dve):
            done = [0]
            near_mark = [0] * T

            def link(ins):
                done[0] += 1
                ins.then_inc(dve_self, 1)
                dve.wait_ge(dve_self, done[0])

            def stats(src, st, mv, ready):
                for t in range(T):
                    last = nc.vector.bn_stats(st[:, t, :], src[:, t, :])
                link(last)
                for t in range(T):
                    last = nc.vector.bn_aggr(mv[:, t, :], st[:, t, :])
                last.then_inc(ready, 1)

            def norm1(b):
                dve.wait_ge(x_in[b], 16)
                if b >= 2:
                    dve.wait_ge(norm1_done, b - 1)
                stats(x_sb[:, b], st1[b % 2], mv1[b % 2], stats1_ready)

            def score_stats(b):
                for t in range(T):
                    dve.wait_ge(sim_copied, T * b + t + 1)
                    last = nc.vector.bn_stats(st0[:, t, :], scores[b % 2][:, t, :])
                link(last)
                for t in range(T):
                    last = nc.vector.bn_aggr(mv0[:, t, :], st0[:, t, :])
                last.then_inc(stats0_ready, 1)

            def drop_above(b):
                dve.wait_ge(pivot_ready, b + 1)
                for t in range(T):
                    last = nc.vector.tensor_scalar(over[:, t, :], scores[b % 2][:, t, :], pivot[:, t:t + 1], 0.0,
                                                   ALU.is_gt, ALU.add, accum_out=count[:, t:t + 1])
                link(last)
                link(nc.vector.scalar_tensor_tensor(left[:, :, :], over[:, :, :], LOWEST, scores[b % 2][:, :, :],
                                                    ALU.mult, ALU.add))

            def take_near(b, r):
                for t in range(T):
                    if r > 0:
                        dve.wait_ge(dve_self, near_mark[t])
                        nc.vector.match_replace(out=left[:, t, :], in_to_replace=near[:, t, 8 * r - 8:8 * r],
                                                in_values=left[:, t, :], imm_value=LOWEST).then_inc(dve_self, 1)
                        done[0] += 1
                        near_mark[t] = done[0]
                for t in range(T):
                    if r > 0:
                        dve.wait_ge(dve_self, near_mark[t])
                    nc.vector.max(near[:, t, 8 * r:8 * r + 8], left[:, t, :]).then_inc(dve_self, 1)
                    done[0] += 1
                    near_mark[t] = done[0]

            def pick_kth(b):
                dve.wait_ge(dve_self, near_mark[T - 1])
                dve.wait_ge(above_ready, 1)
                link(nc.vector.tensor_tensor(place[:, :, :], above[:, :, :],
                                             count[:, :].unsqueeze(2).broadcast_to([P, T, WINDOW]), ALU.is_equal))
                if b >= 1:
                    dve.wait_ge(hits_ready, b)
                nc.vector.tensor_reduce(hit[:, :], place[:, :, :], axis=mybir.AxisListType.XY, op=ALU.add)\
                    .then_inc(hit_ready, 1)
                last = nc.vector.tensor_tensor(kth_pick[:, :, :], near[:, :, :], place[:, :, :], ALU.mult)
                link(last)
                link(nc.vector.tensor_reduce(kth[:, :], kth_pick[:, :, :], axis=mybir.AxisListType.X, op=ALU.add))

            def check_hits(b):
                dve.wait_ge(hits_ready, b + 1)
                nc.vector.tensor_copy(hits[:, :], ps_c[0:1, 0:1]).then_inc(hits_taken, 1)
                dve.wait_ge(hits_taken, b + 1)
                all_hits = dve.value_load(hits[0:1, 0:1], min_val=0, max_val=N)
                with dve.If(all_hits < N):
                    n = 0
                    for r in range(ROUNDS):
                        src = scores[b % 2] if r == 0 else left
                        for t in range(T):
                            if r > 0:
                                dve.wait_ge(fallback[b], n - 1)
                            nc.vector.max(top8[:, t, :], src[:, t, :]).then_inc(fallback[b], 1)
                            n += 1
                        if r == ROUNDS - 1:
                            break
                        for t in range(T):
                            dve.wait_ge(fallback[b], n - 1)
                            nc.vector.match_replace(out=left[:, t, :], in_to_replace=top8[:, t, :],
                                                    in_values=src[:, t, :], imm_value=LOWEST)\
                                .then_inc(fallback[b], 1)
                            n += 1
                    dve.wait_ge(fallback[b], n)
                    nc.vector.tensor_copy(kth[:, :], top8[:, :, KTH]).then_inc(fallback[b], 1)
                    dve.wait_ge(fallback[b], n + 1)

            def mask(b):
                dve.wait_ge(sig_ready, b + 1)
                for t in range(T):
                    nc.vector.scalar_tensor_tensor(masked[:, t, :], scores[b % 2][:, t, :], kth[:, t:t + 1],
                                                   sig[b % 2][:, t, :], ALU.is_ge, ALU.mult).then_inc(masked_ready, 1)

            def lower_up0():
                dve.wait_ge(w_hi, 1)
                nc.vector.tensor_tensor(up_lo[:, 0], up_raw[:, 0], up_hi[:, 0].bitcast(F32),
                                        ALU.subtract).then_inc(up_lo0_ready, 1)

            def lower_down0():
                dve.wait_ge(w_hi, 2)
                nc.vector.tensor_tensor(dn_lo[:, 0], dn_raw[:, 0], dn_hi[:, 0].bitcast(F32),
                                        ALU.subtract).then_inc(dn_lo0_ready, 1)

            def residual1(b):
                dve.wait_ge(maskT_ready, b + 1)
                dve.wait_ge(base_ready, b + 1)
                if b >= 2:
                    dve.wait_ge(fin_ready, b - 1)
                nc.vector.tensor_tensor(x1[b % 2][:, :, :], base[:, :, :],
                                        ps_a[:, :].rearrange("p (t n) -> p t n", t=T), ALU.add).then_inc(x1_ready, 1)
                dve.wait_ge(x1_ready, b + 1)
                stats(x1[b % 2], st2, mv2, stats2_ready)

            def norm2(b):
                dve.wait_ge(rs2_ready, b + 1)
                dve.wait_ge(stats2_ready, b + 1)
                for t in range(T):
                    nc.vector.tensor_scalar(z[:, t, :], x1[b % 2][:, t, :], mv2[:, t, 0:1], rs2[:, t:t + 1],
                                            ALU.subtract, ALU.mult).then_inc(z_ready, 1)

            def low_z(b):
                dve.wait_ge(zhi_ready, b + 1)
                nc.vector.tensor_tensor(z_lo[b % 2][:, :, :], ps_b[:, :].rearrange("p (k n) -> p k n", k=KD),
                                        z_hi[b % 2][:, :, :].bitcast(F32), ALU.subtract).then_inc(zlo_ready, 1)

            def route_a(b):
                if b == 0:
                    dve.wait_ge(consts_ready, 1)
                dve.wait_ge(logits_ready, b + 1)
                link(nc.vector.tensor_copy(lgp[:, :, :, :],
                                           ps_a[:, 0:T * 2 * E].rearrange("p (t a e) -> p t a e", t=T, a=2)))
                link(nc.vector.tensor_tensor(lgx[:, :, 0:E], lgp[:, :, 0, :], lgp[:, :, 1, :], ALU.add))
                for t in range(T):
                    last = nc.vector.max(lg8[:, t, :], lgx[:, t, 0:E])
                link(last)
                nc.vector.tensor_copy(take[:, :, 0:2], lg8[:, :, 0:2]).then_inc(dve_self, 1)
                done[0] += 1
                if b >= 1:
                    dve.wait_ge(exp_ready, b)
                nc.vector.tensor_tensor(lgd[:, :, :], lgx[:, :, 0:E], lg8[:, :, 0:1].broadcast_to([P, T, E]),
                                        ALU.subtract).then_inc(lgd_ready, 1)
                dve.wait_ge(dve_self, done[0])
                for t in range(T):
                    last = nc.vector.match_replace(out=rest[:, t, :], in_to_replace=take[:, t, :],
                                                   in_values=lgx[:, t, :], imm_value=LOWEST)
                link(last)
                link(nc.vector.tensor_tensor(chosen[:, :, :], lgx[:, :, 0:E], rest[:, :, 0:E], ALU.not_equal))

            def route_b(b):
                dve.wait_ge(exp_ready, b + 1)
                nc.vector.tensor_reduce(exs[:, :], ex[:, :, :], axis=mybir.AxisListType.X, op=ALU.add)\
                    .then_inc(dve_self, 1)
                done[0] += 1
                nc.vector.tensor_tensor(exc[:, :, :], ex[:, :, :], chosen[:, :, :], ALU.mult)
                dve.wait_ge(dve_self, done[0])
                link(nc.vector.reciprocal(exr[:, :], exs[:, :]))
                link(nc.vector.tensor_tensor(comb[:, :, :], exc[:, :, :],
                                             exr[:, :].unsqueeze(2).broadcast_to([P, T, E]), ALU.mult))
                link(nc.vector.tensor_copy(comb_r[:, :, 0, :], comb[:, :, :]))
                nc.vector.tensor_tensor(comb_r[:, :, 1, :], comb[:, :, :], comb_r[:, :, 0, :].bitcast(F32),
                                        ALU.subtract).then_inc(comb_ready, 1)

            def gate_values(b, s):
                i = SLOTS * b + s
                w = N * len(experts_of(s))
                dve.wait_ge(silu_ready, i + 1)
                dve.wait_ge(u_ready, i + 1)
                if s == 0:
                    if i >= 2:
                        dve.wait_ge(glo_ready, i - 1)
                    nc.vector.tensor_tensor(gc[i % 2][:, :w], sil[i % 2][:, :w], ps_u[i % 2][:, :w],
                                            ALU.mult).then_inc(prod_ready, 1)
                else:
                    if 4 * b + s > 2:
                        dve.wait_ge(gc_ready, 4 * b + max(s - 2, 0))
                    nc.vector.tensor_tensor(prod[i % 2][:, :w], sil[i % 2][:, :w], ps_u[i % 2][:, :w],
                                            ALU.mult).then_inc(prod_ready, 1)

            def weigh_values(b, s):
                i = SLOTS * b + s
                if i >= 2:
                    dve.wait_ge(glo_ready, i - 1)
                dve.wait_ge(prod_ready, i + 1)
                dve.wait_ge(spread_ready, 4 * b + s)
                nc.vector.tensor_tensor(gc[i % 2][:, :], prod[i % 2][:, :], ps_c[:, :], ALU.mult).then_inc(gc_ready, 1)

            def low_g(b, s):
                i = SLOTS * b + s
                dve.wait_ge(gc_ready, 4 * b + s)
                dve.wait_ge(ghi_ready, i + 1)
                nc.vector.tensor_tensor(g_lo[i % 3][:, :], gc[i % 2][:, :], g_hi[i % 3][:, :].bitcast(F32),
                                        ALU.subtract).then_inc(glo_last, 1)

            def residual2(b):
                dve.wait_ge(down_done, SLOTS * (b + 1))
                nc.vector.tensor_tensor(fin[b][:, :, :], x1[b % 2][:, :, :],
                                        ps_y[:, :].rearrange("p (t d) -> p t d", t=T), ALU.add).then_inc(fin_ready, 1)

            def gamma_parts():
                dve.wait_ge(gamma_tanh, 1)
                nc.vector.tensor_scalar(g_rest[:, :], g_tanh[:, :], -0.5, 0.5, ALU.mult, ALU.add)
                nc.vector.tensor_scalar(g_quarter[:, :], g_tanh[:, :], 0.125, 0.125, ALU.mult, ALU.add)\
                    .then_inc(gamma_ready, 1)

            def lower_gate():
                dve.wait_ge(gate_hi, 1)
                nc.vector.tensor_tensor(gate_r[:, :, 1, :], gate_sb[:, :, :], gate_r[:, :, 0, :].bitcast(F32),
                                        ALU.subtract).then_inc(gate_ready, 1)

            score_stats(0)
            gamma_parts()
            norm1(0)
            norm1(1)
            lower_up0()
            drop_above(0)
            take_near(0, 0)
            take_near(0, 1)
            take_near(0, 2)
            pick_kth(0)
            check_hits(0)
            mask(0)
            score_stats(1)
            residual1(0)
            lower_gate()
            norm2(0)
            low_z(0)
            drop_above(1)
            take_near(1, 0)
            gate_values(0, 0)
            for b in range(B):
                route_a(b)
                if b + 1 < B:
                    take_near(b + 1, 1)
                    take_near(b + 1, 2)
                    pick_kth(b + 1)
                gate_values(b, 1)
                if b >= 1:
                    residual2(b - 1)
                route_b(b)
                if b + 1 < B:
                    check_hits(b + 1)
                    mask(b + 1)
                gate_values(b, 2)
                if b == 0:
                    lower_down0()
                weigh_values(b, 1)
                if b + 1 < B:
                    residual1(b + 1)
                weigh_values(b, 2)
                gate_values(b, 3)
                if b + 1 < B:
                    norm2(b + 1)
                if b + 2 < B:
                    score_stats(b + 2)
                weigh_values(b, 3)
                gate_values(b, 4)
                if b + 1 < B:
                    low_z(b + 1)
                weigh_values(b, 4)
                if b + 2 < B:
                    norm1(b + 2)
                    drop_above(b + 2)
                if b + 1 < B:
                    gate_values(b + 1, 0)
                if b + 2 < B:
                    take_near(b + 2, 0)
            low_g(B - 1, SLOTS - 1)
            residual2(B - 1)
        @block.tensor
        def _(pe):
            def keep_warm(n):
                pe.wait_ge(ident_ready, 2)
                for _ in range(n):
                    nc.tensor.matmul(ps_y[:, 0:P], ident[:, :], ident[:, :], start=True, stop=True)

            def project(b):
                if b == 0:
                    pe.wait_ge(ctx0_in, 32)
                else:
                    pe.wait_ge(ctx_in, 16)
                    pe.wait_ge(tanh_ready, b)
                    if b >= 2:
                        pe.wait_ge(zlo_ready, b - 1)
                nc.tensor.matmul(ps_b[:, 0:N], wqk_sb[:, :, :].rearrange("p a c -> p (a c)"),
                                 ctx_sb[:, b * N:(b + 1) * N], start=True, stop=True).then_inc(qk_ready, 1)

            def similar(b):
                pe.wait_ge(qk_copied, 2 * b + 2)
                for t in range(T):
                    last = nc.tensor.matmul(ps_b[:, t * N:(t + 1) * N], qkT[:, 0, t * P:(t + 1) * P], qkT[:, 1, :],
                                            start=True, stop=True)
                last.then_inc(sim_ready, 1)

            def sum_hits(b):
                if b >= 2:
                    pe.wait_ge(gc_ready, 4 * (b - 1))
                pe.wait_ge(ident_ready, 2)
                pe.wait_ge(above_ready, 1)
                pe.wait_ge(hit_ready, b + 1)
                nc.tensor.matmul(ps_c[0:1, 0:1], ones[:, :], hit[:, :], start=True, stop=True).then_inc(hits_ready, 1)

            def transpose_masked(b):
                for t in range(T):
                    pe.wait_ge(masked_ready, T * b + t + 1)
                    for j in range(T):
                        last = nc.tensor.transpose(ps_a[:, j * N + t * P:j * N + (t + 1) * P],
                                                   masked[:, t, j * P:(j + 1) * P], ident[:, :])
                last.then_inc(maskT_ready, 1)

            def transpose_z(b):
                pe.wait_ge(tanh_ready, min(b + 2, B))
                for t in range(T):
                    pe.wait_ge(z_ready, T * b + t + 1)
                    for k in range(KD):
                        last = nc.tensor.transpose(ps_b[:, k * N + t * P:k * N + (t + 1) * P],
                                                   z[:, t, k * P:(k + 1) * P], ident[:, :])
                last.then_inc(zT_ready, 1)

            def logits(b):
                pe.wait_ge(zhi_ready, b + 1)
                if b == 0:
                    pe.wait_ge(gate_ready, 1)
                pe.wait_ge(zlo_ready, b + 1)
                pe.wait_ge(x1_ready, b + 1)
                n = 0
                for zz in (z_hi, z_lo):
                    for k in range(KD):
                        last = nc.tensor.matmul(ps_a[0:2 * E, 0:N], gate_r[:, k, :, :].rearrange("p a e -> p (a e)"),
                                                zz[b % 2][:, k, :], start=(n == 0), stop=(n == 2 * KD - 1))
                        n += 1
                last.then_inc(lgT_ready, 1)

            def transpose_logits(b):
                pe.wait_ge(lgT_copied, b + 1)
                for t in range(T):
                    last = nc.tensor.transpose(ps_a[:, t * 2 * E:(t + 1) * 2 * E], lgT[:, t * P:(t + 1) * P],
                                               ident[0:2 * E, 0:2 * E])
                last.then_inc(logits_ready, 1)

            def transpose_comb(b):
                pe.wait_ge(comb_ready, b + 1)
                for t in range(T):
                    last = nc.tensor.transpose(ps_a[0:2 * E, t * P:(t + 1) * P],
                                               comb_r[:, t, :, :].rearrange("p a e -> p (a e)").bitcast(F32),
                                               ident[:, :])
                last.then_inc(combT_ready, 1)

            def up(b, s):
                i = SLOTS * b + s
                if s == 0:
                    pe.wait_ge(zhi_ready, b + 1)
                if b == 0:
                    pe.wait_ge(w_hi, 2 * s + 2)
                    if s == 0:
                        pe.wait_ge(up_lo0_ready, 1)
                    else:
                        pe.wait_ge(up_lo_ready, s)
                if i >= 2:
                    pe.wait_ge(silu_ready, i - 1)
                    pe.wait_ge(prod_ready, i - 1)
                for a, (bank, ready) in enumerate(((ps_h, h_ready), (ps_u, u_ready))):
                    for n, e in enumerate(experts_of(s)):
                        dst = bank[i % 2][:, n * N:(n + 1) * N]
                        m = 0
                        for w, zz in ((up_hi, z_hi), (up_lo, z_hi), (up_hi, z_lo)):
                            if zz is z_lo:
                                pe.wait_ge(zlo_ready, b + 1)
                            for k in range(KD):
                                last = nc.tensor.matmul(dst, w[:, e, a, k, :], zz[b % 2][:, k, :],
                                                        start=(m == 0), stop=(m == 3 * KD - 1))
                                m += 1
                    last.then_inc(ready, 1)

            def spread(b, s):
                if s == 1:
                    pe.wait_ge(combT_copied, b + 1)
                    pe.wait_ge(hits_taken, min(b + 2, B))
                if b == 0 and s == 1:
                    pe.wait_ge(pick_rounded, 1)
                if b > 0 or s > 1:
                    pe.wait_ge(gc_ready, 4 * b + s - 1)
                for n in range(2):
                    last = nc.tensor.matmul(ps_c[:, n * N:(n + 1) * N], pick_r[:, 2 * s - 2 + n, :], combT[:, :],
                                            start=True, stop=True)
                last.then_inc(spread_ready, 1)

            def down(b, s):
                i = SLOTS * b + s
                if s == 0 and b >= 1:
                    pe.wait_ge(fin_ready, b)
                if b == 0 and s == 0:
                    pe.wait_ge(dn_lo0_ready, 1)
                elif b == 0:
                    pe.wait_ge(dn_lo_ready, s)
                pe.wait_ge(ghi_ready, i + 1)
                if i == SLOTS * B - 1:
                    pe.wait_ge(glo_last, 1)
                else:
                    pe.wait_ge(glo_ready, i + 1)
                for n, e in enumerate(experts_of(s)):
                    for t in range(T):
                        tok = slice(n * N + t * P, n * N + (t + 1) * P)
                        for m, (g, w) in enumerate(((g_hi, dn_hi), (g_hi, dn_lo), (g_lo, dn_hi))):
                            last = nc.tensor.matmul(ps_y[:, t * D:(t + 1) * D], g[i % 3][:, tok], w[:, e, :],
                                                    start=(s == 0 and t == 0 and m == 0),
                                                    stop=(s == SLOTS - 1 and n == 1 and m == 2),
                                                    skip_group_check=True)
                last.then_inc(down_done, 1)

            keep_warm(7)
            project(0)
            keep_warm(6)
            similar(0)
            project(1)
            similar(1)
            sum_hits(0)
            transpose_masked(0)
            keep_warm(15)
            transpose_z(0)
            for b in range(B):
                if b >= 1:
                    down(b - 1, 2)
                up(b, 0)
                logits(b)
                if b + 2 < B:
                    project(b + 2)
                if b >= 1:
                    down(b - 1, 3)
                transpose_logits(b)
                up(b, 1)
                if b + 2 < B:
                    similar(b + 2)
                up(b, 2)
                if b >= 1:
                    down(b - 1, 4)
                if b + 1 < B:
                    sum_hits(b + 1)
                up(b, 3)
                transpose_comb(b)
                spread(b, 1)
                if b + 1 < B:
                    transpose_masked(b + 1)
                down(b, 0)
                spread(b, 2)
                up(b, 4)
                spread(b, 3)
                down(b, 1)
                if b + 1 < B:
                    transpose_z(b + 1)
                spread(b, 4)
            down(B - 1, 2)
            down(B - 1, 3)
            down(B - 1, 4)


def kernel(**inputs):
    import numpy as np
    import concourse.bacc as bacc
    from concourse.bass_utils import run_bass_kernel_spmd

    f = {k: np.asarray(v) for k, v in inputs.items()}

    def up_layout(w):
        e = w.shape[0]
        return w.transpose(2, 0, 1).reshape(KD, P, e, INTER).transpose(1, 2, 0, 3)

    arrays = {
        "x": f["x"],
        "ctxT": f["ctx_512"].transpose(2, 0, 1).reshape(DC, B * N),
        "wqkT": np.stack([f["L0_xattn_Wq"].T, f["L0_xattn_Wk"].T], axis=1),
        "gamma": f["L0_xattn_gamma_raw"].reshape(1),
        "gateT": f["L0_ffn_gate_w"].T.reshape(KD, P, E).transpose(1, 0, 2),
        "w1t": up_layout(f["L0_ffn_w1"]),
        "w3t": up_layout(f["L0_ffn_w3"]),
        "w2t": f["L0_ffn_w2"].transpose(2, 0, 1),
        "ws1t": up_layout(f["L0_ffn_ws1"][None])[:, 0],
        "ws3t": up_layout(f["L0_ffn_ws3"][None])[:, 0],
        "ws2t": f["L0_ffn_ws2"].T,
    }
    arrays = {f"in_{k}": np.ascontiguousarray(v) for k, v in arrays.items()}
    nc = bacc.Bacc("TRN2", target_bir_lowering=False, num_devices=1)
    args = [nc.dram_tensor(k, v.shape, mybir.dt.from_np(v.dtype), kind="ExternalInput").ap()
            for k, v in arrays.items()]
    args.append(nc.dram_tensor("out_x", (B, N, D), F32, kind="ExternalOutput").ap())
    attention_ffn(nc, *args)
    r = run_bass_kernel_spmd(nc, [arrays], core_ids=[0])
    return r.results[0]["out_x"]
```

```python
import concourse.bass as bass
from concourse import mybir
from contextlib import ExitStack

F32 = mybir.dt.float32
F32R = mybir.dt.float32r
ALU = mybir.AluOpType
ACT = mybir.ActivationFunctionType

P = 128
B = 4
LAST = B - 1
N = 256
D = 256
DC = 64
HEADS = 4
T = N // P
KD = D // P
E = 8
INTER = 128
TOPK = int(N * 0.3)
SIM_SCALE = 1.0 / (float(DC // HEADS) ** 0.5 * HEADS)
LOWEST = -3.0e38
ROUNDS = (TOPK + 7) // 8
KTH = (TOPK - 1) % 8
WINDOW = 24
AIM = TOPK - WINDOW // 2 - 1
FIRST_PIVOT = 0.6
DENSITY = 118.0
FILL = 6
SLOTS = 1 + E // 2


def experts_of(slot):
    return [0] if slot == 0 else [2 * slot - 1, 2 * slot]


def attention_ffn(nc, x, ctxT, wqkT, gamma, gateT, w1t, w3t, w2t, ws1t, ws3t, ws2t, out):
    es = ExitStack()
    with es:
        def sb(name, shape, dt=F32):
            return es.enter_context(nc.sbuf_tensor(name, shape, dt))

        def pb(name):
            return es.enter_context(nc.psum_tensor(name, [P, 512], F32))

        def sem(name):
            return es.enter_context(nc.semaphore(name))

        x_sb = sb("x_sb", [P, B, T, D])
        ctx_sb = sb("ctx_sb", [DC, B * N])
        wqk_sb = sb("wqk_sb", [DC, 2, DC])
        gamma_sb = sb("gamma_sb", [P, 1])
        gate_sb = sb("gate_sb", [P, KD, E])
        gate_r = sb("gate_r", [P, KD, 2, E], F32R)
        up_raw = sb("up_raw", [P, 1 + E, 2, KD, INTER])
        up_hi = sb("up_hi", [P, 1 + E, 2, KD, INTER], F32R)
        up_lo = sb("up_lo", [P, 1 + E, 2, KD, INTER], F32R)
        dn_raw = sb("dn_raw", [P, 1 + E, D])
        dn_hi = sb("dn_hi", [P, 1 + E, D], F32R)
        dn_lo = sb("dn_lo", [P, 1 + E, D], F32R)
        ident = sb("ident", [P, P])
        pick = sb("pick", [2 * E, E, P])
        pick_r = sb("pick_r", [2 * E, E, P], F32R)
        minus_half = sb("minus_half", [P, T])
        plus_half = sb("plus_half", [P, T])
        ones = sb("ones", [P, 1])
        above = sb("above", [P, T, WINDOW])
        euler = sb("euler", [P, T, E])
        g_tanh = sb("g_tanh", [P, 1])
        g_rest = sb("g_rest", [P, 1])
        g_quarter = sb("g_quarter", [P, 1])

        qkT = [sb(f"qkT_{b}", [DC, 2, N]) for b in range(B)]
        scores = [sb(f"scores_{b}", [P, T, N]) for b in range(B)]
        left = sb("left", [P, T, N])
        top8 = sb("top8", [P, T, 8])
        st0 = [sb(f"st0_{b}", [P, T, 6]) for b in range(B)]
        mv0 = [sb(f"mv0_{b}", [P, T, 2]) for b in range(B)]
        dev = [sb(f"dev_{b}", [P, T]) for b in range(B)]
        step = [sb(f"step_{b}", [P, T]) for b in range(B)]
        offset = [sb(f"offset_{b}", [P, T]) for b in range(B)]
        neg_pivot = [sb(f"neg_pivot_{b}", [P, T]) for b in range(B)]
        sides = [sb(f"sides{t}", [P, N]) for t in range(T)]
        balance = [sb(f"balance_{b}", [P, T]) for b in range(B)]
        excess = [sb(f"excess_{b}", [P, T]) for b in range(B)]
        pivot = [sb(f"pivot_{b}", [P, T]) for b in range(B)]
        delta = [sb(f"delta_{b}", [P, T]) for b in range(B)]
        first_delta = sb("first_delta", [P, T])
        count = sb("count", [P, T])
        over = sb("over", [P, T, N])
        near = sb("near", [P, T, WINDOW])
        place = sb("place", [P, T, WINDOW])
        hit = sb("hit", [P, 1])
        hits = sb("hits", [1, 1], mybir.dt.int32)
        kth_pick = sb("kth_pick", [P, T, WINDOW])
        kth = sb("kth", [P, T])
        sig = [sb(f"sig_{b}", [P, T, N]) for b in range(B)]
        masked = sb("masked", [P, T, N])
        st1 = [sb(f"st1_{b}", [P, T, 6]) for b in range(B)]
        mv1 = [sb(f"mv1_{b}", [P, T, 2]) for b in range(B)]
        var1 = sb("var1", [P, T])
        rs1 = sb("rs1", [P, T])
        c1 = sb("c1", [P, T])
        sc1 = sb("sc1", [P, T])
        mc1 = sb("mc1", [P, T])
        bi1 = sb("bi1", [P, T])
        ln1 = sb("ln1", [P, T, N])
        base = sb("base", [P, T, N])
        x1 = [sb(f"x1_{i}", [P, T, D]) for i in range(2)]
        st2 = sb("st2", [P, T, 6])
        mv2 = sb("mv2", [P, T, 2])
        var2 = sb("var2", [P, T])
        rs2 = sb("rs2", [P, T])
        z = sb("z", [P, T, D])
        z_hi = [sb(f"z_hi{i}", [P, KD, N], F32R) for i in range(2)]
        z_lo = [sb(f"z_lo{i}", [P, KD, N], F32R) for i in range(2)]

        lgx = sb("lgx", [P, T, E + FILL])
        lgT = sb("lgT", [2 * E, N])
        lgp = sb("lgp", [P, T, 2, E])
        lg8 = sb("lg8", [P, T, 8])
        take = sb("take", [P, T, 8])
        rest = sb("rest", [P, T, E + FILL])
        lgd = sb("lgd", [P, T, E])
        ex = sb("ex", [P, T, E])
        exs = sb("exs", [P, T])
        exr = sb("exr", [P, T])
        chosen = sb("chosen", [P, T, E])
        exc = sb("exc", [P, T, E])
        comb = sb("comb", [P, T, E])
        comb_r = sb("comb_r", [P, T, 2, E], F32R)
        combT = sb("combT", [2 * E, N], F32R)

        sil = [sb(f"sil{i}", [P, 512]) for i in range(2)]
        prod = [sb(f"prod{i}", [P, 512]) for i in range(2)]
        gc = [sb(f"gc{i}", [P, 512]) for i in range(2)]
        g_hi = [sb(f"g_hi{i}", [P, 512], F32R) for i in range(3)]
        g_lo = [sb(f"g_lo{i}", [P, 512], F32R) for i in range(3)]
        fin = [sb(f"fin_{b}", [P, T, D]) for b in range(B)]

        ps_a = pb("ps_a")
        ps_b = pb("ps_b")
        ps_h = [pb("ps_h0"), pb("ps_h1")]
        ps_u = [pb("ps_u0"), pb("ps_u1")]
        ps_c = pb("ps_c")
        ps_y = pb("ps_y")
        ps_qk = [ps_h[0], ps_h[1], ps_u[0], ps_a]
        ps_sim = [ps_b, ps_y, ps_h[0], ps_h[1]]

        ctx0_in = sem("ctx0_in")
        ctx_in = sem("ctx_in")
        x_in = [sem(f"x_in{b}") for b in range(B)]
        gamma_in = sem("gamma_in")
        gate_in = sem("gate_in")
        w_in = [sem(f"w_in{s}") for s in range(SLOTS)]
        pool_self = sem("pool_self")
        dve_self = sem("dve_self")
        ident_ready = sem("ident_ready")
        pick_ready = sem("pick_ready")
        pick_rounded = sem("pick_rounded")
        consts_ready = sem("consts_ready")
        above_ready = sem("above_ready")
        gamma_tanh = sem("gamma_tanh")
        gamma_ready = sem("gamma_ready")
        gate_hi = sem("gate_hi")
        gate_ready = sem("gate_ready")
        w_hi = sem("w_hi")
        up_lo0_ready = sem("up_lo0_ready")
        dn_lo0_ready = sem("dn_lo0_ready")
        up_lo_ready = sem("up_lo_ready")
        dn_lo_ready = sem("dn_lo_ready")
        qk_ready = sem("qk_ready")
        qk_copied = sem("qk_copied")
        sim_ready = sem("sim_ready")
        sim_copied = sem("sim_copied")
        tanh_ready = sem("tanh_ready")
        sig_ready = sem("sig_ready")
        stats0_ready = sem("stats0_ready")
        pivot0_ready = sem("pivot0_ready")
        balance_ready = sem("balance_ready")
        pivot_ready = sem("pivot_ready")
        hit_ready = sem("hit_ready")
        hits_ready = sem("hits_ready")
        hits_taken = sem("hits_taken")
        fallback = [sem(f"fallback{b}") for b in range(B)]
        lgT_ready = sem("lgT_ready")
        lgT_copied = sem("lgT_copied")
        stats1_ready = sem("stats1_ready")
        norm1_done = sem("norm1_done")
        base_ready = sem("base_ready")
        masked_ready = sem("masked_ready")
        maskT_ready = sem("maskT_ready")
        x1_ready = sem("x1_ready")
        stats2_ready = sem("stats2_ready")
        rs2_ready = sem("rs2_ready")
        z_ready = sem("z_ready")
        zT_ready = sem("zT_ready")
        zhi_ready = sem("zhi_ready")
        zlo_ready = sem("zlo_ready")
        logits_ready = sem("logits_ready")
        lgd_ready = sem("lgd_ready")
        exp_ready = sem("exp_ready")
        comb_ready = sem("comb_ready")
        combT_ready = sem("combT_ready")
        combT_copied = sem("combT_copied")
        h_ready = sem("h_ready")
        u_ready = sem("u_ready")
        silu_ready = sem("silu_ready")
        prod_ready = sem("prod_ready")
        spread_ready = sem("spread_ready")
        gc_ready = sem("gc_ready")
        ghi_ready = sem("ghi_ready")
        glo_ready = sem("glo_ready")
        gc_last = sem("gc_last")
        ghi_last = sem("ghi_last")
        glo_last = sem("glo_last")
        down_done = sem("down_done")
        fin_ready = sem("fin_ready")
        out_done = sem("out_done")

        block = es.enter_context(nc.Block())

        @block.sync
        def _(sp):
            sp.dma_start(ctx_sb[:, 0:N], ctxT[:, 0:N]).then_inc(ctx0_in, 16)
            sp.dma_start(ctx_sb[:, N:], ctxT[:, N:]).then_inc(ctx_in, 16)
            sp.dma_start(x_sb[:, 0, :, :], x[0].rearrange("(t p) d -> p t d", p=P)).then_inc(x_in[0], 16)
            sp.dma_start(x_sb[:, 1, :, :], x[1].rearrange("(t p) d -> p t d", p=P)).then_inc(x_in[1], 16)
            sp.dma_start(up_raw[:, 0, 0, :, :], ws1t).then_inc(w_in[0], 16)
            sp.dma_start(up_raw[:, 0, 1, :, :], ws3t).then_inc(w_in[0], 16)
            sp.dma_start(dn_raw[:, 0, :], ws2t).then_inc(w_in[0], 16)
            for s in range(1, SLOTS):
                e = 2 * s - 2
                sp.dma_start(up_raw[:, 1 + e:3 + e, 0, :, :], w1t[:, e:e + 2, :, :]).then_inc(w_in[s], 16)
                sp.dma_start(up_raw[:, 1 + e:3 + e, 1, :, :], w3t[:, e:e + 2, :, :]).then_inc(w_in[s], 16)
                sp.dma_start(dn_raw[:, 1 + e:3 + e, :], w2t[:, e:e + 2, :]).then_inc(w_in[s], 16)
            for b in range(2, B):
                sp.dma_start(x_sb[:, b, :, :], x[b].rearrange("(t p) d -> p t d", p=P)).then_inc(x_in[b], 16)
            for b in range(B):
                sp.wait_ge(fin_ready, b + 1)
                sp.dma_start(out[b].rearrange("(t p) d -> p t d", p=P), fin[b][:, :, :]).then_inc(out_done, 16)
            sp.wait_ge(out_done, 16 * B)

        @block.gpsimd
        def _(pool):
            done = [0]

            def link(ins):
                done[0] += 1
                ins.then_inc(pool_self, 1)
                pool.wait_ge(pool_self, done[0])

            def lower_up(s):
                a, z_ = 2 * s - 1, 2 * s + 1
                pool.wait_ge(w_hi, 2 * s + 1)
                nc.gpsimd.tensor_tensor(up_lo[:, a:z_], up_raw[:, a:z_], up_hi[:, a:z_].bitcast(F32),
                                        ALU.subtract).then_inc(up_lo_ready, 1)

            def lower_down(s):
                a, z_ = 2 * s - 1, 2 * s + 1
                pool.wait_ge(w_hi, 2 * s + 2)
                nc.gpsimd.tensor_tensor(dn_lo[:, a:z_], dn_raw[:, a:z_], dn_hi[:, a:z_].bitcast(F32),
                                        ALU.subtract).then_inc(dn_lo_ready, 1)

            def norm1(b):
                pool.wait_ge(stats1_ready, b + 1)
                link(nc.gpsimd.tensor_scalar(var1[:, :], mv1[b][:, :, 1], 1e-5, None, ALU.add))
                link(nc.gpsimd.tensor_tensor(rs1[:, :], var1[:, :], minus_half[:, :], ALU.pow))
                if b == 0:
                    pool.wait_ge(gamma_ready, 1)
                link(nc.gpsimd.tensor_scalar(c1[:, :], rs1[:, :], g_rest[:, 0:1], None, ALU.mult))
                nc.gpsimd.tensor_scalar(sc1[:, :], c1[:, :], 1.0, None, ALU.add)
                link(nc.gpsimd.tensor_tensor(mc1[:, :], mv1[b][:, :, 0], c1[:, :], ALU.mult))
                link(nc.gpsimd.tensor_scalar(bi1[:, :], mc1[:, :], -1.0, None, ALU.mult))
                for t in range(T):
                    last = nc.gpsimd.tensor_scalar(ln1[:, t, :], x_sb[:, b, t, :], sc1[:, t:t + 1],
                                                   bi1[:, t:t + 1], ALU.mult, ALU.add)
                last.then_inc(norm1_done, 1)

            def deviation0():
                pool.wait_ge(stats0_ready, 1)
                link(nc.gpsimd.tensor_tensor(dev[0][:, :], mv0[0][:, :, 1], plus_half[:, :], ALU.pow))
                nc.gpsimd.tensor_scalar(step[0][:, :], dev[0][:, :], 1.0 / DENSITY, None, ALU.mult).then_inc(pivot0_ready, 1)

            def first_pivot(b):
                pool.wait_ge(stats0_ready, b + 1)
                link(nc.gpsimd.tensor_tensor(dev[b][:, :], mv0[b][:, :, 1], plus_half[:, :], ALU.pow))
                nc.gpsimd.tensor_scalar(step[b][:, :], dev[b][:, :], 0.5 / DENSITY, None, ALU.mult)
                link(nc.gpsimd.tensor_scalar(offset[b][:, :], dev[b][:, :], -FIRST_PIVOT, None, ALU.mult))
                nc.gpsimd.tensor_tensor(neg_pivot[b][:, :], offset[b][:, :], mv0[b][:, :, 0], ALU.subtract)\
                    .then_inc(pivot0_ready, 1)

            def second_pivot(b):
                pool.wait_ge(balance_ready, b)
                link(nc.gpsimd.tensor_scalar(excess[b][:, :], balance[b][:, :], float(N - 2 * AIM), None, ALU.add))
                link(nc.gpsimd.tensor_tensor(delta[b][:, :], excess[b][:, :], step[b][:, :], ALU.mult))
                nc.gpsimd.tensor_tensor(pivot[b][:, :], delta[b][:, :], neg_pivot[b][:, :], ALU.subtract)\
                    .then_inc(pivot_ready, 1)

            def sigmoid(b):
                pool.wait_ge(tanh_ready, b + 1)
                nc.gpsimd.tensor_scalar(sig[b][:, :, :], sig[b][:, :, :], g_quarter[:, 0:1], g_quarter[:, 0:1],
                                        ALU.mult, ALU.add).then_inc(sig_ready, 1)

            def add_masked(b):
                pool.wait_ge(norm1_done, b + 1)
                pool.wait_ge(masked_ready, T * (b + 1))
                nc.gpsimd.tensor_tensor(base[:, :, :], ln1[:, :, :], masked[:, :, :],
                                        ALU.add).then_inc(base_ready, 1)

            def norm2(b):
                pool.wait_ge(stats2_ready, b + 1)
                link(nc.gpsimd.tensor_scalar(var2[:, :], mv2[:, :, 1], 1e-5, None, ALU.add))
                nc.gpsimd.tensor_tensor(rs2[:, :], var2[:, :], minus_half[:, :], ALU.pow).then_inc(rs2_ready, 1)

            def exps(b):
                pool.wait_ge(lgd_ready, b + 1)
                nc.gpsimd.tensor_tensor(ex[:, :, :], euler[:, :, :], lgd[:, :, :], ALU.pow).then_inc(exp_ready, 1)

            def low_g(b, s):
                i = SLOTS * b + s
                w = N * len(experts_of(s))
                pool.wait_ge(ghi_ready, i + 1)
                nc.gpsimd.tensor_tensor(g_lo[i % 3][:, :w], gc[i % 2][:, :w], g_hi[i % 3][:, :w].bitcast(F32),
                                        ALU.subtract).then_inc(glo_ready, 1)

            nc.gpsimd.memset(plus_half[:, :], 0.5)
            nc.gpsimd.memset(minus_half[:, :], -0.5)
            nc.gpsimd.memset(ident[:, :], 0.0).then_inc(ident_ready, 1)
            pool.wait_ge(ident_ready, 1)
            nc.gpsimd.affine_select(out=ident[:, :], in_=ident[:, :], compare_op=ALU.not_equal, fill=1.0, base=0,
                                    pattern=[[-1, P]], channel_multiplier=1).then_inc(ident_ready, 1)
            nc.gpsimd.memset(ones[:, :], 1.0)
            nc.gpsimd.iota(above[:, :, :], pattern=[[0, T], [-1, WINDOW]], base=TOPK - 1, channel_multiplier=0,
                           allow_small_or_imprecise_dtypes=True).then_inc(above_ready, 1)
            nc.gpsimd.memset(euler[:, :, :], 2.718281828459045)
            nc.gpsimd.memset(lgx[:, :, :], LOWEST)
            nc.gpsimd.memset(take[:, :, :], LOWEST).then_inc(consts_ready, 1)
            link(nc.gpsimd.memset(pick[:, :, :], 0.0))
            for half in range(2):
                last = nc.gpsimd.affine_select(out=pick[:, :, :], in_=pick[:, :, :], compare_op=ALU.not_equal,
                                               fill=1.0, base=-E * half, pattern=[[-1, E], [0, P]],
                                               channel_multiplier=1)
                if half == 0:
                    link(last)
            last.then_inc(pick_ready, 1)
            deviation0()
            norm1(0)
            sigmoid(0)
            lower_up(1)
            lower_up(2)
            lower_up(3)
            lower_down(1)
            norm2(0)
            first_pivot(1)
            sigmoid(1)
            sigmoid(2)
            second_pivot(1)
            first_pivot(2)
            lower_up(4)
            first_pivot(3)
            exps(0)
            norm1(1)
            second_pivot(2)
            low_g(0, 0)
            second_pivot(3)
            add_masked(1)
            low_g(0, 1)
            lower_down(2)
            norm2(1)
            low_g(0, 2)
            low_g(0, 3)
            lower_down(3)
            lower_down(4)
            low_g(0, 4)
            low_g(1, 0)
            exps(1)
            sigmoid(3)
            norm1(2)
            add_masked(2)
            low_g(1, 1)
            norm2(2)
            low_g(1, 2)
            for b in range(1, LAST):
                low_g(b, 3)
                if b + 2 < B:
                    norm1(b + 2)
                low_g(b, 4)
                exps(b + 1)
                low_g(b + 1, 0)
                if b + 2 < B:
                    add_masked(b + 2)
                low_g(b + 1, 1)
                if b + 2 < B:
                    norm2(b + 2)
                low_g(b + 1, 2)
            low_g(LAST, 3)
        @block.scalar
        def _(act):
            act.dma_start(wqk_sb[:, :, :], wqkT).then_inc(ctx0_in, 16)
            nc.scalar.preload_act_table(ACT.Silu)
            act.dma_start(gamma_sb[:, :], gamma.partition_broadcast(P)).then_inc(gamma_in, 16)
            act.dma_start(gate_sb[:, :, :], gateT).then_inc(gate_in, 16)

            def upper_parts(s):
                ps = experts_of(s)
                a, z_ = ps[0], ps[-1] + 1
                act.wait_ge(w_in[s], 48)
                nc.scalar.activation(up_hi[:, a:z_], up_raw[:, a:z_], ACT.Copy).then_inc(w_hi, 1)
                nc.scalar.activation(dn_hi[:, a:z_], dn_raw[:, a:z_], ACT.Copy).then_inc(w_hi, 1)

            def copy_qk(b):
                act.wait_ge(qk_ready, b + 1)
                for a in range(2):
                    nc.scalar.activation(qkT[b][:, a, :], ps_qk[b][a * DC:(a + 1) * DC, 0:N], ACT.Copy)\
                        .then_inc(qk_copied, 1)

            def copy_scores(b):
                v = ps_sim[b][:, :].rearrange("p (t n) -> p t n", t=T)
                for t in range(T):
                    act.wait_ge(sim_ready, b + 1)
                    nc.scalar.activation(scores[b][:, t, :], v[:, t, :], ACT.Copy).then_inc(sim_copied, 1)
                nc.scalar.activation(sig[b][:, :, :], v, ACT.Tanh, scale=SIM_SCALE / 2).then_inc(tanh_ready, 1)

            def balance_scores(b):
                act.wait_ge(pivot0_ready, b + 1)
                if b >= 2:
                    act.wait_ge(balance_ready, b - 1)
                for t in range(T):
                    last = nc.scalar.activation(sides[t][:, :], scores[b][:, t, :], ACT.Sign,
                                                bias=neg_pivot[b][:, t:t + 1], accum_out=balance[b][:, t:t + 1])
                last.then_inc(balance_ready, 1)

            def high_z(b):
                act.wait_ge(zT_ready, b + 1)
                if b >= 2:
                    act.wait_ge(u_ready, SLOTS * (b - 1))
                nc.scalar.activation(z_hi[b % 2][:, :, :], ps_b[:, :].rearrange("p (k n) -> p k n", k=KD),
                                     ACT.Copy).then_inc(zhi_ready, 1)

            def copy_logits(b):
                act.wait_ge(lgT_ready, b + 1)
                nc.scalar.activation(lgT[:, :], ps_a[0:2 * E, 0:N], ACT.Copy).then_inc(lgT_copied, 1)

            def copy_combT(b):
                act.wait_ge(combT_ready, b + 1)
                if b >= 1:
                    act.wait_ge(spread_ready, 4 * b)
                nc.scalar.activation(combT[:, :], ps_a[0:2 * E, 0:N], ACT.Copy).then_inc(combT_copied, 1)

            def silu(b, s):
                i = SLOTS * b + s
                w = N * len(experts_of(s))
                act.wait_ge(h_ready, i + 1)
                if i >= 2:
                    act.wait_ge(prod_ready, i - 1)
                nc.scalar.activation(sil[i % 2][:, :w], ps_h[i % 2][:, :w], ACT.Silu).then_inc(silu_ready, 1)

            def high_g(b, s):
                i = SLOTS * b + s
                w = N * len(experts_of(s))
                if s == 0:
                    act.wait_ge(prod_ready, i + 1)
                else:
                    act.wait_ge(gc_ready, 4 * b + s)
                if i >= 3:
                    act.wait_ge(down_done, i - 2)
                nc.scalar.activation(g_hi[i % 3][:, :w], gc[i % 2][:, :w], ACT.Copy).then_inc(ghi_ready, 1)

            def tanh_gamma():
                act.wait_ge(gamma_in, 16)
                nc.scalar.activation(g_tanh[:, :], gamma_sb[:, :], ACT.Tanh, scale=0.5).then_inc(gamma_tanh, 1)

            def upper_gate():
                act.wait_ge(gate_in, 16)
                nc.scalar.activation(gate_r[:, :, 0, :], gate_sb[:, :, :], ACT.Copy).then_inc(gate_hi, 1)

            def round_pick():
                act.wait_ge(pick_ready, 1)
                nc.scalar.activation(pick_r[:, :, :], pick[:, :, :], ACT.Copy).then_inc(pick_rounded, 1)

            def high_last(n):
                i, cols = SLOTS * B - 1, slice(n * N, (n + 1) * N)
                act.wait_ge(gc_last, n + 1)
                act.wait_ge(down_done, i - 2)
                nc.scalar.activation(g_hi[i % 3][:, cols], gc[i % 2][:, cols], ACT.Copy).then_inc(ghi_last, 1)

            tanh_gamma()
            copy_qk(0)
            copy_scores(0)
            upper_gate()
            upper_parts(0)
            copy_qk(1)
            upper_parts(1)
            copy_qk(2)
            copy_scores(1)
            round_pick()
            upper_parts(2)
            copy_scores(2)
            upper_parts(3)
            copy_qk(3)
            copy_scores(3)
            high_z(0)
            balance_scores(1)
            upper_parts(4)
            copy_logits(0)
            silu(0, 0)
            balance_scores(2)
            silu(0, 1)
            silu(0, 2)
            balance_scores(3)
            high_g(0, 0)
            copy_combT(0)
            high_g(0, 1)
            silu(0, 3)
            silu(0, 4)
            high_g(0, 2)
            high_z(1)
            high_g(0, 3)
            silu(1, 0)
            for b in range(1, LAST):
                high_g(b - 1, 4)
                high_g(b, 0)
                silu(b, 1)
                copy_logits(b)
                silu(b, 2)
                silu(b, 3)
                copy_combT(b)
                high_g(b, 1)
                high_g(b, 2)
                silu(b, 4)
                high_g(b, 3)
                high_z(b + 1)
                silu(b + 1, 0)
            high_g(LAST - 1, 4)
            copy_logits(LAST)
            silu(LAST, 1)
            silu(LAST, 2)
            high_g(LAST, 0)
            copy_combT(LAST)
            high_g(LAST, 1)
            silu(LAST, 3)
            silu(LAST, 4)
            high_g(LAST, 2)
            high_g(LAST, 3)
            high_last(0)
            high_last(1)
        @block.vector
        def _(dve):
            done = [0]
            near_mark = [0] * T

            def link(ins):
                done[0] += 1
                ins.then_inc(dve_self, 1)
                dve.wait_ge(dve_self, done[0])

            def stats(src, st, mv, ready):
                for t in range(T):
                    last = nc.vector.bn_stats(st[:, t, :], src[:, t, :])
                link(last)
                for t in range(T):
                    last = nc.vector.bn_aggr(mv[:, t, :], st[:, t, :])
                last.then_inc(ready, 1)

            def norm1(b):
                dve.wait_ge(x_in[b], 16)
                stats(x_sb[:, b], st1[b], mv1[b], stats1_ready)

            def score_stats(b):
                for t in range(T):
                    dve.wait_ge(sim_copied, T * b + t + 1)
                    last = nc.vector.bn_stats(st0[b][:, t, :], scores[b][:, t, :])
                link(last)
                for t in range(T):
                    last = nc.vector.bn_aggr(mv0[b][:, t, :], st0[b][:, t, :])
                last.then_inc(stats0_ready, 1)

            def pivots0():
                dve.wait_ge(pivot0_ready, 1)
                link(nc.vector.scalar_tensor_tensor(pivot[0][:, :], dev[0][:, :], FIRST_PIVOT, mv0[0][:, :, 0],
                                                    ALU.mult, ALU.add))
                for t in range(T):
                    last = nc.vector.tensor_scalar(over[:, t, :], scores[0][:, t, :], pivot[0][:, t:t + 1], 0.0,
                                                   ALU.is_gt, ALU.add, accum_out=count[:, t:t + 1])
                link(last)
                link(nc.vector.scalar_tensor_tensor(first_delta[:, :], count[:, :], float(AIM), step[0][:, :],
                                                    ALU.subtract, ALU.mult))
                nc.vector.tensor_tensor(pivot[0][:, :], pivot[0][:, :], first_delta[:, :], ALU.add).then_inc(pivot_ready, 1)

            def drop_above(b):
                dve.wait_ge(pivot_ready, b + 1)
                for t in range(T):
                    last = nc.vector.tensor_scalar(over[:, t, :], scores[b][:, t, :], pivot[b][:, t:t + 1], 0.0,
                                                   ALU.is_gt, ALU.add, accum_out=count[:, t:t + 1])
                link(last)
                link(nc.vector.scalar_tensor_tensor(left[:, :, :], over[:, :, :], LOWEST, scores[b][:, :, :],
                                                    ALU.mult, ALU.add))

            def take_near(b, r):
                for t in range(T):
                    if r > 0:
                        dve.wait_ge(dve_self, near_mark[t])
                        nc.vector.match_replace(out=left[:, t, :], in_to_replace=near[:, t, 8 * r - 8:8 * r],
                                                in_values=left[:, t, :], imm_value=LOWEST).then_inc(dve_self, 1)
                        done[0] += 1
                        near_mark[t] = done[0]
                for t in range(T):
                    if r > 0:
                        dve.wait_ge(dve_self, near_mark[t])
                    nc.vector.max(near[:, t, 8 * r:8 * r + 8], left[:, t, :]).then_inc(dve_self, 1)
                    done[0] += 1
                    near_mark[t] = done[0]

            def pick_kth(b):
                dve.wait_ge(dve_self, near_mark[T - 1])
                dve.wait_ge(above_ready, 1)
                link(nc.vector.tensor_tensor(place[:, :, :], above[:, :, :],
                                             count[:, :].unsqueeze(2).broadcast_to([P, T, WINDOW]), ALU.is_equal))
                if b >= 1:
                    dve.wait_ge(hits_ready, b)
                nc.vector.tensor_reduce(hit[:, :], place[:, :, :], axis=mybir.AxisListType.XY, op=ALU.add)\
                    .then_inc(hit_ready, 1)
                last = nc.vector.tensor_tensor(kth_pick[:, :, :], near[:, :, :], place[:, :, :], ALU.mult)
                link(last)
                link(nc.vector.tensor_reduce(kth[:, :], kth_pick[:, :, :], axis=mybir.AxisListType.X, op=ALU.add))

            def check_hits(b):
                dve.wait_ge(hits_ready, b + 1)
                nc.vector.tensor_copy(hits[:, :], ps_c[0:1, 0:1]).then_inc(hits_taken, 1)
                dve.wait_ge(hits_taken, b + 1)
                all_hits = dve.value_load(hits[0:1, 0:1], min_val=0, max_val=N)
                with dve.If(all_hits < N):
                    n = 0
                    for r in range(ROUNDS):
                        src = scores[b] if r == 0 else left
                        for t in range(T):
                            if r > 0:
                                dve.wait_ge(fallback[b], n - 1)
                            nc.vector.max(top8[:, t, :], src[:, t, :]).then_inc(fallback[b], 1)
                            n += 1
                        if r == ROUNDS - 1:
                            break
                        for t in range(T):
                            dve.wait_ge(fallback[b], n - 1)
                            nc.vector.match_replace(out=left[:, t, :], in_to_replace=top8[:, t, :],
                                                    in_values=src[:, t, :], imm_value=LOWEST)\
                                .then_inc(fallback[b], 1)
                            n += 1
                    dve.wait_ge(fallback[b], n)
                    nc.vector.tensor_copy(kth[:, :], top8[:, :, KTH]).then_inc(fallback[b], 1)
                    dve.wait_ge(fallback[b], n + 1)

            def mask(b):
                dve.wait_ge(sig_ready, b + 1)
                for t in range(T):
                    nc.vector.scalar_tensor_tensor(masked[:, t, :], scores[b][:, t, :], kth[:, t:t + 1],
                                                   sig[b][:, t, :], ALU.is_ge, ALU.mult).then_inc(masked_ready, 1)

            def add_masked0():
                dve.wait_ge(norm1_done, 1)
                dve.wait_ge(masked_ready, T)
                nc.vector.tensor_tensor(base[:, :, :], ln1[:, :, :], masked[:, :, :], ALU.add).then_inc(base_ready, 1)

            def lower_up0():
                dve.wait_ge(w_hi, 1)
                nc.vector.tensor_tensor(up_lo[:, 0], up_raw[:, 0], up_hi[:, 0].bitcast(F32),
                                        ALU.subtract).then_inc(up_lo0_ready, 1)

            def lower_down0():
                dve.wait_ge(w_hi, 2)
                nc.vector.tensor_tensor(dn_lo[:, 0], dn_raw[:, 0], dn_hi[:, 0].bitcast(F32),
                                        ALU.subtract).then_inc(dn_lo0_ready, 1)

            def residual1(b):
                dve.wait_ge(maskT_ready, b + 1)
                dve.wait_ge(base_ready, b + 1)
                if b >= 2:
                    dve.wait_ge(fin_ready, b - 1)
                nc.vector.tensor_tensor(x1[b % 2][:, :, :], base[:, :, :],
                                        ps_a[:, :].rearrange("p (t n) -> p t n", t=T), ALU.add).then_inc(x1_ready, 1)
                dve.wait_ge(x1_ready, b + 1)
                stats(x1[b % 2], st2, mv2, stats2_ready)

            def norm2(b):
                dve.wait_ge(rs2_ready, b + 1)
                dve.wait_ge(stats2_ready, b + 1)
                for t in range(T):
                    nc.vector.tensor_scalar(z[:, t, :], x1[b % 2][:, t, :], mv2[:, t, 0:1], rs2[:, t:t + 1],
                                            ALU.subtract, ALU.mult).then_inc(z_ready, 1)

            def low_z(b):
                dve.wait_ge(zhi_ready, b + 1)
                nc.vector.tensor_tensor(z_lo[b % 2][:, :, :], ps_b[:, :].rearrange("p (k n) -> p k n", k=KD),
                                        z_hi[b % 2][:, :, :].bitcast(F32), ALU.subtract).then_inc(zlo_ready, 1)

            def route_a(b):
                if b == 0:
                    dve.wait_ge(consts_ready, 1)
                dve.wait_ge(logits_ready, b + 1)
                link(nc.vector.tensor_copy(lgp[:, :, :, :],
                                           ps_a[:, 0:T * 2 * E].rearrange("p (t a e) -> p t a e", t=T, a=2)))
                link(nc.vector.tensor_tensor(lgx[:, :, 0:E], lgp[:, :, 0, :], lgp[:, :, 1, :], ALU.add))
                for t in range(T):
                    last = nc.vector.max(lg8[:, t, :], lgx[:, t, 0:E])
                link(last)
                nc.vector.tensor_copy(take[:, :, 0:2], lg8[:, :, 0:2]).then_inc(dve_self, 1)
                done[0] += 1
                if b >= 1:
                    dve.wait_ge(exp_ready, b)
                nc.vector.tensor_tensor(lgd[:, :, :], lgx[:, :, 0:E], lg8[:, :, 0:1].broadcast_to([P, T, E]),
                                        ALU.subtract).then_inc(lgd_ready, 1)
                dve.wait_ge(dve_self, done[0])
                for t in range(T):
                    last = nc.vector.match_replace(out=rest[:, t, :], in_to_replace=take[:, t, :],
                                                   in_values=lgx[:, t, :], imm_value=LOWEST)
                link(last)
                link(nc.vector.tensor_tensor(chosen[:, :, :], lgx[:, :, 0:E], rest[:, :, 0:E], ALU.not_equal))

            def route_b(b):
                dve.wait_ge(exp_ready, b + 1)
                nc.vector.tensor_reduce(exs[:, :], ex[:, :, :], axis=mybir.AxisListType.X, op=ALU.add)\
                    .then_inc(dve_self, 1)
                done[0] += 1
                nc.vector.tensor_tensor(exc[:, :, :], ex[:, :, :], chosen[:, :, :], ALU.mult)
                dve.wait_ge(dve_self, done[0])
                link(nc.vector.reciprocal(exr[:, :], exs[:, :]))
                link(nc.vector.tensor_tensor(comb[:, :, :], exc[:, :, :],
                                             exr[:, :].unsqueeze(2).broadcast_to([P, T, E]), ALU.mult))
                link(nc.vector.tensor_copy(comb_r[:, :, 0, :], comb[:, :, :]))
                nc.vector.tensor_tensor(comb_r[:, :, 1, :], comb[:, :, :], comb_r[:, :, 0, :].bitcast(F32),
                                        ALU.subtract).then_inc(comb_ready, 1)

            def gate_values(b, s):
                i = SLOTS * b + s
                w = N * len(experts_of(s))
                dve.wait_ge(silu_ready, i + 1)
                dve.wait_ge(u_ready, i + 1)
                if s == 0:
                    if i >= 2:
                        dve.wait_ge(glo_ready, i - 1)
                    nc.vector.tensor_tensor(gc[i % 2][:, :w], sil[i % 2][:, :w], ps_u[i % 2][:, :w],
                                            ALU.mult).then_inc(prod_ready, 1)
                else:
                    if 4 * b + s > 2:
                        dve.wait_ge(gc_ready, 4 * b + max(s - 2, 0))
                    nc.vector.tensor_tensor(prod[i % 2][:, :w], sil[i % 2][:, :w], ps_u[i % 2][:, :w],
                                            ALU.mult).then_inc(prod_ready, 1)

            def weigh_values(b, s):
                i = SLOTS * b + s
                if i >= 2:
                    dve.wait_ge(glo_ready, i - 1)
                dve.wait_ge(prod_ready, i + 1)
                dve.wait_ge(spread_ready, 4 * b + s)
                nc.vector.tensor_tensor(gc[i % 2][:, :], prod[i % 2][:, :], ps_c[:, :], ALU.mult).then_inc(gc_ready, 1)

            def weigh_last(n):
                i, cols = SLOTS * B - 1, slice(n * N, (n + 1) * N)
                dve.wait_ge(glo_ready, i - 1)
                dve.wait_ge(prod_ready, i + 1)
                dve.wait_ge(spread_ready, 4 * B)
                nc.vector.tensor_tensor(gc[i % 2][:, cols], prod[i % 2][:, cols], ps_c[:, cols],
                                        ALU.mult).then_inc(gc_last, 1)

            def low_last(n):
                i, cols = SLOTS * B - 1, slice(n * N, (n + 1) * N)
                dve.wait_ge(gc_last, n + 1)
                dve.wait_ge(ghi_last, n + 1)
                nc.vector.tensor_tensor(g_lo[i % 3][:, cols], gc[i % 2][:, cols], g_hi[i % 3][:, cols].bitcast(F32),
                                        ALU.subtract).then_inc(glo_last, 1)

            def residual2(b):
                dve.wait_ge(down_done, SLOTS * (b + 1))
                nc.vector.tensor_tensor(fin[b][:, :, :], x1[b % 2][:, :, :],
                                        ps_y[:, :].rearrange("p (t d) -> p t d", t=T), ALU.add).then_inc(fin_ready, 1)

            def gamma_parts():
                dve.wait_ge(gamma_tanh, 1)
                nc.vector.tensor_scalar(g_rest[:, :], g_tanh[:, :], -0.5, 0.5, ALU.mult, ALU.add)
                nc.vector.tensor_scalar(g_quarter[:, :], g_tanh[:, :], 0.125, 0.125, ALU.mult, ALU.add)\
                    .then_inc(gamma_ready, 1)

            def lower_gate():
                dve.wait_ge(gate_hi, 1)
                nc.vector.tensor_tensor(gate_r[:, :, 1, :], gate_sb[:, :, :], gate_r[:, :, 0, :].bitcast(F32),
                                        ALU.subtract).then_inc(gate_ready, 1)

            gamma_parts()
            norm1(0)
            norm1(1)
            score_stats(0)
            lower_up0()
            pivots0()
            drop_above(0)
            take_near(0, 0)
            take_near(0, 1)
            take_near(0, 2)
            pick_kth(0)
            check_hits(0)
            mask(0)
            lower_gate()
            add_masked0()
            residual1(0)
            score_stats(1)
            norm2(0)
            score_stats(2)
            low_z(0)
            score_stats(3)
            drop_above(1)
            lower_down0()
            route_a(0)
            gate_values(0, 0)
            take_near(1, 0)
            take_near(1, 1)
            gate_values(0, 1)
            take_near(1, 2)
            route_b(0)
            pick_kth(1)
            gate_values(0, 2)
            check_hits(1)
            mask(1)
            weigh_values(0, 1)
            weigh_values(0, 2)
            residual1(1)
            gate_values(0, 3)
            weigh_values(0, 3)
            norm2(1)
            gate_values(0, 4)
            norm1(2)
            low_z(1)
            weigh_values(0, 4)
            drop_above(2)
            gate_values(1, 0)
            for b in range(1, LAST):
                take_near(b + 1, 0)
                take_near(b + 1, 1)
                route_a(b)
                take_near(b + 1, 2)
                gate_values(b, 1)
                pick_kth(b + 1)
                route_b(b)
                check_hits(b + 1)
                mask(b + 1)
                residual2(b - 1)
                gate_values(b, 2)
                weigh_values(b, 1)
                residual1(b + 1)
                weigh_values(b, 2)
                gate_values(b, 3)
                norm2(b + 1)
                weigh_values(b, 3)
                gate_values(b, 4)
                if b + 2 < B:
                    norm1(b + 2)
                low_z(b + 1)
                if b + 2 < B:
                    drop_above(b + 2)
                weigh_values(b, 4)
                gate_values(b + 1, 0)
            route_a(LAST)
            gate_values(LAST, 1)
            route_b(LAST)
            weigh_values(LAST, 1)
            gate_values(LAST, 2)
            residual2(LAST - 1)
            weigh_values(LAST, 2)
            gate_values(LAST, 3)
            weigh_values(LAST, 3)
            gate_values(LAST, 4)
            weigh_last(0)
            weigh_last(1)
            low_last(0)
            low_last(1)
            residual2(LAST)
        @block.tensor
        def _(pe):
            def keep_warm(n):
                pe.wait_ge(ident_ready, 2)
                for _ in range(n):
                    nc.tensor.matmul(ps_u[1][:, 0:P], ident[:, :], ident[:, :], start=True, stop=True)

            def project(b):
                if b == 0:
                    pe.wait_ge(ctx0_in, 32)
                else:
                    pe.wait_ge(ctx_in, 16)
                nc.tensor.matmul(ps_qk[b][:, 0:N], wqk_sb[:, :, :].rearrange("p a c -> p (a c)"),
                                 ctx_sb[:, b * N:(b + 1) * N], start=True, stop=True).then_inc(qk_ready, 1)

            def similar(b):
                pe.wait_ge(qk_copied, 2 * b + 2)
                for t in range(T):
                    last = nc.tensor.matmul(ps_sim[b][:, t * N:(t + 1) * N], qkT[b][:, 0, t * P:(t + 1) * P],
                                            qkT[b][:, 1, :], start=True, stop=True)
                last.then_inc(sim_ready, 1)

            def sum_hits(b):
                if b >= 2:
                    pe.wait_ge(gc_ready, 4 * (b - 1))
                pe.wait_ge(ident_ready, 2)
                pe.wait_ge(above_ready, 1)
                pe.wait_ge(hit_ready, b + 1)
                nc.tensor.matmul(ps_c[0:1, 0:1], ones[:, :], hit[:, :], start=True, stop=True).then_inc(hits_ready, 1)

            def transpose_masked(b):
                if b == 0:
                    pe.wait_ge(qk_copied, 2 * B)
                for t in range(T):
                    pe.wait_ge(masked_ready, T * b + t + 1)
                    for j in range(T):
                        last = nc.tensor.transpose(ps_a[:, j * N + t * P:j * N + (t + 1) * P],
                                                   masked[:, t, j * P:(j + 1) * P], ident[:, :])
                last.then_inc(maskT_ready, 1)

            def transpose_z(b):
                if b == 0:
                    pe.wait_ge(tanh_ready, 1)
                else:
                    pe.wait_ge(zlo_ready, b)
                for t in range(T):
                    pe.wait_ge(z_ready, T * b + t + 1)
                    for k in range(KD):
                        last = nc.tensor.transpose(ps_b[:, k * N + t * P:k * N + (t + 1) * P],
                                                   z[:, t, k * P:(k + 1) * P], ident[:, :])
                last.then_inc(zT_ready, 1)

            def logits(b):
                pe.wait_ge(zhi_ready, b + 1)
                if b == 0:
                    pe.wait_ge(gate_ready, 1)
                pe.wait_ge(zlo_ready, b + 1)
                pe.wait_ge(x1_ready, b + 1)
                n = 0
                for zz in (z_hi, z_lo):
                    for k in range(KD):
                        last = nc.tensor.matmul(ps_a[0:2 * E, 0:N], gate_r[:, k, :, :].rearrange("p a e -> p (a e)"),
                                                zz[b % 2][:, k, :], start=(n == 0), stop=(n == 2 * KD - 1))
                        n += 1
                last.then_inc(lgT_ready, 1)

            def transpose_logits(b):
                pe.wait_ge(lgT_copied, b + 1)
                for t in range(T):
                    last = nc.tensor.transpose(ps_a[:, t * 2 * E:(t + 1) * 2 * E], lgT[:, t * P:(t + 1) * P],
                                               ident[0:2 * E, 0:2 * E])
                last.then_inc(logits_ready, 1)

            def transpose_comb(b):
                pe.wait_ge(comb_ready, b + 1)
                for t in range(T):
                    last = nc.tensor.transpose(ps_a[0:2 * E, t * P:(t + 1) * P],
                                               comb_r[:, t, :, :].rearrange("p a e -> p (a e)").bitcast(F32),
                                               ident[:, :])
                last.then_inc(combT_ready, 1)

            def up(b, s):
                i = SLOTS * b + s
                if s == 0:
                    pe.wait_ge(zhi_ready, b + 1)
                if i < 2:
                    pe.wait_ge(tanh_ready, i + 3)
                if b == 0:
                    pe.wait_ge(w_hi, 2 * s + 2)
                    if s == 0:
                        pe.wait_ge(up_lo0_ready, 1)
                    else:
                        pe.wait_ge(up_lo_ready, s)
                if i >= 2:
                    pe.wait_ge(silu_ready, i - 1)
                    pe.wait_ge(prod_ready, i - 1)
                for a, (bank, ready) in enumerate(((ps_h, h_ready), (ps_u, u_ready))):
                    for n, e in enumerate(experts_of(s)):
                        dst = bank[i % 2][:, n * N:(n + 1) * N]
                        m = 0
                        for w, zz in ((up_hi, z_hi), (up_lo, z_hi), (up_hi, z_lo)):
                            if zz is z_lo:
                                pe.wait_ge(zlo_ready, b + 1)
                            for k in range(KD):
                                last = nc.tensor.matmul(dst, w[:, e, a, k, :], zz[b % 2][:, k, :],
                                                        start=(m == 0), stop=(m == 3 * KD - 1))
                                m += 1
                    last.then_inc(ready, 1)

            def spread(b, s):
                if s == 1:
                    pe.wait_ge(combT_copied, b + 1)
                    pe.wait_ge(hits_taken, min(b + 2, B))
                if b == 0 and s == 1:
                    pe.wait_ge(pick_rounded, 1)
                if b > 0 or s > 1:
                    pe.wait_ge(gc_ready, 4 * b + s - 1)
                for n in range(2):
                    last = nc.tensor.matmul(ps_c[:, n * N:(n + 1) * N], pick_r[:, 2 * s - 2 + n, :], combT[:, :],
                                            start=True, stop=True)
                last.then_inc(spread_ready, 1)

            def down_expert(i, s, n, e):
                for t in range(T):
                    tok = slice(n * N + t * P, n * N + (t + 1) * P)
                    for m, (g, w) in enumerate(((g_hi, dn_hi), (g_hi, dn_lo), (g_lo, dn_hi))):
                        last = nc.tensor.matmul(ps_y[:, t * D:(t + 1) * D], g[i % 3][:, tok], w[:, e, :],
                                                start=(s == 0 and t == 0 and m == 0),
                                                stop=(s == SLOTS - 1 and n == 1 and m == 2), skip_group_check=True)
                return last

            def down(b, s):
                i = SLOTS * b + s
                if s == 0 and b >= 1:
                    pe.wait_ge(fin_ready, b)
                if b == 0 and s == 0:
                    pe.wait_ge(tanh_ready, 2)
                    pe.wait_ge(dn_lo0_ready, 1)
                elif b == 0:
                    pe.wait_ge(dn_lo_ready, s)
                pe.wait_ge(ghi_ready, i + 1)
                pe.wait_ge(glo_ready, i + 1)
                for n, e in enumerate(experts_of(s)):
                    last = down_expert(i, s, n, e)
                last.then_inc(down_done, 1)

            def down_last():
                for n, e in enumerate(experts_of(SLOTS - 1)):
                    pe.wait_ge(ghi_last, n + 1)
                    pe.wait_ge(glo_last, n + 1)
                    last = down_expert(SLOTS * B - 1, SLOTS - 1, n, e)
                last.then_inc(down_done, 1)

            keep_warm(5)
            project(0)
            keep_warm(2)
            keep_warm(1)
            similar(0)
            project(1)
            project(2)
            keep_warm(2)
            project(3)
            similar(1)
            keep_warm(3)
            similar(2)
            keep_warm(2)
            keep_warm(2)
            keep_warm(7)
            sum_hits(0)
            keep_warm(3)
            transpose_masked(0)
            keep_warm(7)
            similar(3)
            transpose_z(0)
            keep_warm(2)
            logits(0)
            up(0, 0)
            transpose_logits(0)
            keep_warm(5)
            up(0, 1)
            up(0, 2)
            up(0, 3)
            sum_hits(1)
            transpose_comb(0)
            spread(0, 1)
            down(0, 0)
            spread(0, 2)
            transpose_masked(1)
            up(0, 4)
            spread(0, 3)
            down(0, 1)
            transpose_z(1)
            for b in range(1, LAST):
                spread(b - 1, 4)
                down(b - 1, 2)
                up(b, 0)
                logits(b)
                up(b, 1)
                transpose_logits(b)
                down(b - 1, 3)
                up(b, 2)
                down(b - 1, 4)
                sum_hits(b + 1)
                transpose_comb(b)
                up(b, 3)
                spread(b, 1)
                transpose_masked(b + 1)
                down(b, 0)
                spread(b, 2)
                up(b, 4)
                spread(b, 3)
                down(b, 1)
                transpose_z(b + 1)
            spread(LAST - 1, 4)
            down(LAST - 1, 2)
            up(LAST, 0)
            logits(LAST)
            down(LAST - 1, 3)
            transpose_logits(LAST)
            up(LAST, 1)
            up(LAST, 2)
            transpose_comb(LAST)
            down(LAST - 1, 4)
            spread(LAST, 1)
            up(LAST, 3)
            spread(LAST, 2)
            up(LAST, 4)
            spread(LAST, 3)
            down(LAST, 0)
            down(LAST, 1)
            spread(LAST, 4)
            down(LAST, 2)
            down(LAST, 3)
            down_last()


def kernel(**inputs):
    import numpy as np
    import concourse.bacc as bacc
    from concourse.bass_utils import run_bass_kernel_spmd

    f = {k: np.asarray(v) for k, v in inputs.items()}

    def up_layout(w):
        e = w.shape[0]
        return w.transpose(2, 0, 1).reshape(KD, P, e, INTER).transpose(1, 2, 0, 3)

    arrays = {
        "x": f["x"],
        "ctxT": f["ctx_512"].transpose(2, 0, 1).reshape(DC, B * N),
        "wqkT": np.stack([f["L0_xattn_Wq"].T, f["L0_xattn_Wk"].T], axis=1),
        "gamma": f["L0_xattn_gamma_raw"].reshape(1),
        "gateT": f["L0_ffn_gate_w"].T.reshape(KD, P, E).transpose(1, 0, 2),
        "w1t": up_layout(f["L0_ffn_w1"]),
        "w3t": up_layout(f["L0_ffn_w3"]),
        "w2t": f["L0_ffn_w2"].transpose(2, 0, 1),
        "ws1t": up_layout(f["L0_ffn_ws1"][None])[:, 0],
        "ws3t": up_layout(f["L0_ffn_ws3"][None])[:, 0],
        "ws2t": f["L0_ffn_ws2"].T,
    }
    arrays = {f"in_{k}": np.ascontiguousarray(v) for k, v in arrays.items()}
    nc = bacc.Bacc("TRN2", target_bir_lowering=False, num_devices=1)
    args = [nc.dram_tensor(k, v.shape, mybir.dt.from_np(v.dtype), kind="ExternalInput").ap()
            for k, v in arrays.items()]
    args.append(nc.dram_tensor("out_x", (B, N, D), F32, kind="ExternalOutput").ap())
    attention_ffn(nc, *args)
    r = run_bass_kernel_spmd(nc, [arrays], core_ids=[0])
    return r.results[0]["out_x"]
```
